# Optimizing a Trainium2 kernel written in Bass

```python
import numpy as np
import jax
import jax.numpy as jnp

def _softmax(x, axis=-1):
    return jax.nn.softmax(x, axis=axis)
def _gelu(x):
    return jax.nn.gelu(x, approximate=True)
def _silu(x):
    return jax.nn.silu(x)
def _sigmoid(x):
    return jax.nn.sigmoid(x)
def _layernorm(x, axis=-1, eps=1e-5):
    m = jnp.mean(x, axis=axis, keepdims=True)
    v = jnp.var(x, axis=axis, keepdims=True)
    return (x - m) / jnp.sqrt(v + eps)
def _scatter_add(tgt, idx, src, axis=0):
    return tgt.at[idx].add(src)
def _segment_sum(src, seg, n):
    return jax.ops.segment_sum(src, seg, n)

kernel_name = 'mk_adj_resnorm_d2_adj_64_70226c'

def setup_inputs(seed: int = 0):
    np.random.seed(seed)
    _w = jnp.asarray
    def _rec_inputs():
        import jax
        import jax.numpy as jnp
        _gk = jax.random.key(seed)
        x = -9.806e-05 + 1 * jax.random.normal(jax.random.fold_in(_gk, 1), (8192, 64), jnp.float32)
        _a = jax.random.bernoulli(jax.random.fold_in(_gk, 2), 0.000976562, (8192, 8192))
        adj = _a.astype(jnp.int32)
        return x, adj
    x, adj = _rec_inputs()
    def _L0_gnn_setup():
        import jax, jax.numpy as jnp
        import numpy as np
        ALPHA = 0.2
        NEG_BIG = -9000000000000000.0
        key = jax.random.key(seed)
        k1, k2, k3, k4, k5 = jax.random.split(key, 5)
        N, M, F_in, F_out = (8192, 8192, 64, 64)
        item_embs = jax.random.normal(k1, (N, F_in), dtype=jnp.float32)
        entity_embs = jax.random.normal(k2, (M, F_in), dtype=jnp.float32)
        adj = jax.random.randint(k3, (N, M), 0, 2, dtype=jnp.int32)
        W = jax.random.normal(k4, (F_in, F_out), dtype=jnp.float32)
        a = jax.random.normal(k5, (2 * F_out, 1), dtype=jnp.float32)
        return {'item_embs': item_embs, 'entity_embs': entity_embs, 'adj': adj, 'W': W, 'a': a}
    _L0_gnn_all = _L0_gnn_setup()
    _L0_gnn_in = {k: v for k, v in _L0_gnn_all.items() if k in ('entity_embs', 'W', 'a', )}
    del _L0_gnn_all

    def _L1_gnn_setup():
        import jax, jax.numpy as jnp
        import numpy as np
        N = 4096
        C = 64
        GDEP = 2
        HID = 32
        ALPHA = 0.2
        NEG_INF = jnp.float32(-9000000000000000.0)

        def _gat_layer(h, adj_mask, W_l, lw, lb, a):
            Wh = h @ W_l
            L1, L2 = (lw[:C], lw[C:])
            u = Wh @ L1 @ a
            v = Wh @ L2 @ a
            c = lb @ a
            e = jax.nn.leaky_relu(u + v.T + c, negative_slope=ALPHA)
            scores = jnp.where(adj_mask, e, NEG_INF)
            att = jax.nn.softmax(scores, axis=1)
            return jax.nn.elu(att @ Wh)
        key = jax.random.key(seed)
        ks = jax.random.split(key, 8)
        x = jax.random.normal(ks[0], (N, C), jnp.float32)
        adj = jax.random.randint(ks[1], (N, N), 0, 2, jnp.int32)
        W = jax.random.normal(ks[2], (GDEP, C, C), jnp.float32) / np.sqrt(C)
        lin_w = jax.random.normal(ks[3], (GDEP, 2 * C, HID), jnp.float32) / np.sqrt(2 * C)
        lin_b = jnp.zeros((GDEP, HID), jnp.float32)
        attn = jax.random.normal(ks[4], (GDEP, HID, 1), jnp.float32) / np.sqrt(HID)
        mlp_w = jax.random.normal(ks[5], ((GDEP + 1) * C, C), jnp.float32) / np.sqrt((GDEP + 1) * C)
        mlp_b = jnp.zeros((C,), jnp.float32)
        return dict(x=x, adj=adj, W=W, lin_w=lin_w, lin_b=lin_b, attn=attn, mlp_w=mlp_w, mlp_b=mlp_b)
    _L1_gnn_all = _L1_gnn_setup()
    _L1_gnn_in = {k: v for k, v in _L1_gnn_all.items() if k in ('W', 'lin_w', 'lin_b', 'attn', 'mlp_w', 'mlp_b', )}
    del _L1_gnn_all

    return {
        "x": x,
        "adj": adj,
        "L0_gnn_entity_embs": _L0_gnn_in["entity_embs"],
        "L0_gnn_W": _L0_gnn_in["W"],
        "L0_gnn_a": _L0_gnn_in["a"],
        "L1_gnn_W": _L1_gnn_in["W"],
        "L1_gnn_lin_w": _L1_gnn_in["lin_w"],
        "L1_gnn_lin_b": _L1_gnn_in["lin_b"],
        "L1_gnn_attn": _L1_gnn_in["attn"],
        "L1_gnn_mlp_w": _L1_gnn_in["mlp_w"],
        "L1_gnn_mlp_b": _L1_gnn_in["mlp_b"],
    }

def reference(x, adj, L0_gnn_entity_embs, L0_gnn_W, L0_gnn_a, L1_gnn_W, L1_gnn_lin_w, L1_gnn_lin_b, L1_gnn_attn, L1_gnn_mlp_w, L1_gnn_mlp_b):
    import jax
    import jax.numpy as jnp
    def _L0_gnn_ref(item_embs, entity_embs, adj, W, a):
        import jax, jax.numpy as jnp
        import numpy as np
        ALPHA = 0.2
        NEG_BIG = -9000000000000000.0
        F_out = W.shape[1]
        Wh = item_embs @ W
        We = entity_embs @ W
        a1 = a[:F_out, 0]
        a2 = a[F_out:, 0]
        scores = (Wh @ a1)[:, None] + (We @ a2)[None, :]
        e = jnp.where(scores > 0, scores, ALPHA * scores)
        e = jnp.where(adj > 0, e, NEG_BIG)
        attention = jax.nn.softmax(e, axis=1)
        entity_emb_weighted = attention @ entity_embs
        h_prime = entity_emb_weighted + item_embs
        return jax.nn.elu(h_prime)

    def _L1_gnn_ref(x, adj, W, lin_w, lin_b, attn, mlp_w, mlp_b):
        import jax, jax.numpy as jnp
        import numpy as np
        N = 4096
        C = 64
        GDEP = 2
        HID = 32
        ALPHA = 0.2
        NEG_INF = jnp.float32(-9000000000000000.0)

        def _gat_layer(h, adj_mask, W_l, lw, lb, a):
            Wh = h @ W_l
            L1, L2 = (lw[:C], lw[C:])
            u = Wh @ L1 @ a
            v = Wh @ L2 @ a
            c = lb @ a
            e = jax.nn.leaky_relu(u + v.T + c, negative_slope=ALPHA)
            scores = jnp.where(adj_mask, e, NEG_INF)
            att = jax.nn.softmax(scores, axis=1)
            return jax.nn.elu(att @ Wh)
        mask = adj > 0
        h = x
        outs = [h]
        for i in range(GDEP):
            h = ALPHA * x + (1.0 - ALPHA) * _gat_layer(h, mask, W[i], lin_w[i], lin_b[i], attn[i])
            outs.append(h)
        ho = jnp.concatenate(outs, axis=-1)
        return ho @ mlp_w + mlp_b

    x = _layernorm(x + _L0_gnn_ref(x, L0_gnn_entity_embs, adj, L0_gnn_W, L0_gnn_a), axis=-1)
    x = _layernorm(x + _L1_gnn_ref(x, adj, L1_gnn_W, L1_gnn_lin_w, L1_gnn_lin_b, L1_gnn_attn, L1_gnn_mlp_w, L1_gnn_mlp_b), axis=-1)
    return x


_drawn_inputs = setup_inputs


def setup_inputs(seed=0):
    import zlib

    import numpy as np

    out = dict(_drawn_inputs(seed))
    spreads = {'L1_gnn_lin_b': (0.0, 0.1), 'L1_gnn_mlp_b': (0.0, 0.1)}
    factors = {}
    for name, (base, spread) in spreads.items():
        noise = np.random.default_rng([zlib.crc32(name.encode()), seed]).standard_normal(out[name].shape)
        drawn = base * np.exp(spread * noise) if base else spread * noise
        out[name] = jnp.asarray(drawn.astype(out[name].dtype))
    for name, factor in factors.items():
        out[name] = (out[name] * factor).astype(out[name].dtype)
    return out
```

```python
from contextlib import ExitStack

import concourse.bass as bass
from concourse import mybir

ALU = mybir.AluOpType
ACT = mybir.ActivationFunctionType
F32 = mybir.dt.float32
BF16 = mybir.dt.bfloat16
FP8 = mybir.dt.float8e4
I32 = mybir.dt.int32
U8 = mybir.dt.uint8
ONE8 = 56
AX = mybir.AxisListType.X

P = 128
N = 8192
C = 64
HID = 32
CE = C + 1
NT = N // P
BI = 512
RT = BI // P
NB = N // BI
PAIRS = NT // 2
CH = 4
CW = N // CH
UNITS = CH * RT
NLAYER = 3
ALPHA = 0.2
BIG = 9.0e15
EPS = 1e-5
TS = 4
ZS = 2
WC = 2 * C + 2

SEQ_SETUP = 4
SEQ_START = 8
SEQ_HEAD = 9
SEQ_TAIL = (9, 5, 9)

T_EVAC = 3
T_TURN = 4
T_A = 5
T_EXP = 7
T_B = 8
T_C = 10
T_HT = 12
T_HTE = 13
T_OUT = 14
T_OUTE = 15
T_Y = 17
T_D = 19
T_UNITS = 24
T_HEAD = 25
T_HEADT = 27


def unit_slots():
    at = {}
    for u in range(UNITS):
        at.setdefault(u * T_UNITS // UNITS, []).append(u)
    return at


UNIT_AT = unit_slots()
UNIT_AT_0 = {(u + 1) * T_UNITS // UNITS: [u] for u in range(UNITS)}


def build(nc, x, adj, ent, W0, a0, W12, lin_w, lin_b, attn, mlp_w, mlp_b, out):
    with ExitStack() as ctx:
        def sb(name, shape, dt=F32):
            return ctx.enter_context(nc.sbuf_tensor(name, shape, dt))

        def ps(name, shape, dt=F32):
            return ctx.enter_context(nc.psum_tensor(name, shape, dt))

        def sem(name):
            return ctx.enter_context(nc.semaphore(name))

        mask_d = nc.dram_tensor("mask_d", [NB, CH, P, RT * CW], U8).ap()
        uv_d = nc.dram_tensor("uv_d", [NLAYER, 2, N], F32).ap()
        xy_d = nc.dram_tensor("xy_d", [2, N, 2 * C], F32).ap()

        mask = sb("mask", [P, 2, CH, RT, CW], U8)
        stage = sb("stage", [P, RT, CW], I32)
        vw = sb("vw", [P, N])
        feat = sb("feat", [P, 2, NT, CE])
        score = sb("score", [P, TS, 2, BI])
        ub = sb("ub", [P, 2, BI])
        xin = sb("xin", [P, RT, 2 * C])
        acc_s = sb("acc_s", [CE, BI])
        g = sb("g", [P, RT, CE])
        z = sb("z", [P, RT, C])
        e = sb("e", [P, RT, C])
        hn = sb("hn", [P, RT, C])
        ht = sb("ht", [CE, BI])
        uvrow = sb("uvrow", [2, BI])
        pj = sb("pj", [P, RT, C])
        v8col = sb("v8col", [P, 2, NT])
        v2col = sb("v2col", [P, 2, NT])
        ucol = sb("ucol", [P, 2, NT])
        nuv = sb("nuv", [P, NT])
        st = sb("st", [P, 16])
        fsum = sb("fsum", [P, CE])
        pw = sb("pw", [P, RT, CH])
        w4 = sb("w4", [P, RT])
        ns = sb("ns", [P, RT])
        nm = sb("nm", [P, RT])
        r1 = sb("r1", [P, RT])
        emp = sb("emp", [P, 2, RT])
        parts = sb("parts", [P, RT, 4], BF16)
        mrow = sb("mrow", [3, 2, BI], BF16)
        rden = sb("rden", [P, RT])
        mom = sb("mom", [P, RT])
        mom2 = sb("mom2", [P, RT])
        half = sb("half", [P, RT])
        rstd = sb("rstd", [P, RT])
        wcat = sb("wcat", [CE, NLAYER, WC])
        wuv0 = sb("wuv0", [CE, 2])
        wt = sb("wt", [C, NLAYER, CE])
        q = sb("q", [C, NLAYER, 2])
        lin = sb("lin", [C, 2, 2, HID])
        att = sb("att", [C, 2, HID])
        lbx = sb("lbx", [HID, 2, CE])
        attc = sb("attc", [HID, 2, 2])
        wld = xin[0:C, 0:NLAYER, 0:C]
        junk = sb("junk", [P, 2, CW], U8)
        ident = sb("ident", [P, P])
        identb = sb("identb", [P, P], BF16)
        nbig = sb("nbig", [P, P], BF16)
        ones = sb("ones", [P, P])
        ones3 = sb("ones3", [3, P], BF16)

        zps = ps("zps", [P, ZS, 2, BI])
        acc = ps("acc", [P, 2, BI])
        miscA = ps("miscA", [P, BI])
        miscB = ps("miscB", [P, BI])
        miscAb = miscA[:, :].bitcast(BF16)

        s_w = sem("weights_landed")
        s_zero = sem("memsets_done")
        s_const = sem("constants_done")
        s_wt = sem("w_turned")
        s_wte = sem("w_turned_out")
        s_wuv = sem("wuv_done")
        s_wcat = sem("wcat_done")
        s_pin = [sem("prep_ent_landed"), sem("prep_x_landed")]
        s_ptr = sem("prep_turned")
        s_pte = sem("prep_turned_out")
        s_pmm = sem("prep_products")
        s_pout = sem("prep_products_out")
        s_feat0 = sem("entity_features_landed")
        s_vb = sem("v_rows_landed")
        s_uvst = sem("uv_rows_stored")
        s_fsum = sem("feature_sum_done")
        s_fsume = sem("feature_sum_out")
        s_start = sem("layer_start_done")
        s_stage = [sem(f"adjacency_landed{i}") for i in range(RT)]
        s_mask = sem("mask_unit_made")
        s_unit = sem("unit_minimum_done")
        s_mload = [sem(f"mask_loaded{i}") for i in range(2 * CH)]
        s_mst = [sem(f"mask_stored{i}") for i in range(2 * CH)]
        s_ub = [sem("ub_landed0"), sem("ub_landed1")]
        s_xin = sem("xin_landed")
        s_z = sem("z_built")
        s_lr = sem("leaky_done")
        s_add = sem("scores_done")
        s_p = sem("probs_done")
        s_main = sem("probs_used")
        s_setup = sem("setup_steps")
        s_startseq = sem("layer_start_steps")
        s_headseq = sem("head_steps")
        s_tailseq = [sem(f"tail_steps{l}") for l in range(NLAYER)]
        s_split = sem("maxima_split")
        s_mt = sem("maxima_turned")
        s_mte = sem("maxima_rows_out")
        s_acce = sem("sums_out")
        s_gt = sem("sums_turned")
        s_ga = sem("tail_a_done")
        s_ex = sem("tail_exp_done")
        s_mom = sem("variance_done")
        s_rstd = sem("rstd_done")
        s_h = sem("features_done")
        s_htt = sem("features_turned")
        s_hte = sem("features_columns_out")
        s_om = sem("next_products")
        s_oe = sem("next_products_out")
        s_y = sem("output_sums_done")
        s_x1 = sem("x1_stored")
        s_mom2 = sem("last_variance_done")
        s_rstd2 = sem("last_rstd_done")
        s_fin = sem("result_done")
        s_out = sem("result_stored")

        def blk(l, b):
            return l * NB + b

        def pair(l, b, t):
            return (l * NB + b) * PAIRS + t

        def blocks(eng, body):
            body(0, 0, True, False)
            body(1, 1, True, True)
            body(2, 0, True, True)
            with eng.Fori(0, (NB - 4) // 2) as k:
                body(2 * k + 3, 1, True, True)
                body(2 * k + 4, 0, True, True)
            body(NB - 1, 1, False, True)

        adj_v = adj.rearrange("(b r p) (c w) -> b c r p w", r=RT, p=P, w=CW)
        x_v = x.rearrange("(b r p) c -> b p r c", r=RT, p=P)
        ent_v = ent.rearrange("(b r p) c -> b p r c", r=RT, p=P)
        xy_v = xy_d.rearrange("l (b r p) c -> l b p r c", r=RT, p=P)
        out_v = out.rearrange("(b r p) c -> b p r c", r=RT, p=P)

        block = ctx.enter_context(nc.Block())

        @block.sync
        def _(sp):
            n_w = 0

            def w_load(dst, src):
                sp.dma_start(dst, src).then_inc(s_w, 16)

            sp.wait_ge(s_zero, 4)
            w_load(wld[:, 0, :], W0)
            w_load(wld[:, 1:3, :], W12.rearrange("l f g -> f l g"))
            w_load(wcat[0:C, 0:2, 0:C], W12.rearrange("l f g -> f l g"))
            w_load(wcat[0:C, :, C + 2:WC], mlp_w.rearrange("(l f) g -> f l g", l=NLAYER))
            w_load(wcat[C:CE, 0, C + 2:WC], mlp_b.rearrange("(o g) -> o g", o=1))
            with nc.allow_non_contiguous_dma(reason="a few hundred weights"):
                w_load(q[:, 0, 0:1], a0[C:2 * C, :])
                w_load(q[:, 0, 1:2], a0[0:C, :])
                w_load(lin[:, :, :, :], lin_w.rearrange("l (s f) h -> f l s h", s=2))
                for l in range(2):
                    w_load(att[:, l, :], attn[l].rearrange("h o -> o h").broadcast_to([C, HID]))
                    w_load(lbx[:, l, C:CE], lin_b[l].rearrange("(h o) -> h o", o=1))
                    w_load(attc[:, l, 1:2], attn[l])
            sp.dma_start(feat[:, 0, :, 0:C], ent.rearrange("(t p) c -> p t c", p=P)).then_inc(s_feat0, 16)

            def ub_load(l, b, par):
                sp.dma_start(ub[:, par, :], uv_d[l, 1:2, bass.ds(b * BI, BI)].broadcast_to([P, BI])).then_inc(
                    s_ub[par], 16)

            def xin_load(l, b):
                if l == 0:
                    sp.dma_start(xin[:, :, 0:C], x_v[b]).then_inc(s_xin, 16)
                else:
                    sp.dma_start(xin[:, :, :], xy_v[l - 1, b]).then_inc(s_xin, 16)

            def xin_free(l, b):
                if isinstance(b, int) and b == 0 and l != 1:
                    return
                if l < 2:
                    sp.wait_ge(s_x1, 16 * blk(l, b))
                else:
                    sp.wait_ge(s_mom2, b)

            def units(l, b, par):
                for u in range(UNITS):
                    c, r = divmod(u, RT)
                    if l == 0:
                        if not (isinstance(b, int) and b == 0 and c == 0):
                            sp.wait_ge(s_mask, blk(0, b) * UNITS + u - RT + 1)
                        sp.dma_start(stage[:, r, :], adj_v[b, c, r]).then_inc(s_stage[r], 16)
                        if r == RT - 1 and c > 0:
                            store(b, c - 1, par)
                    elif r == 0:
                        sp.dma_start(mask[:, par, c, :, :].rearrange("p r w -> p (r w)"),
                                     mask_d[b, c]).then_inc(s_mload[par * CH + c], 16)
                if l == 0:
                    store(b, CH - 1, par)

            def store(b, c, par):
                sp.wait_ge(s_mask, (b * CH + c + 1) * RT)
                sp.dma_start(mask_d[b, c], mask[:, par, c, :, :].rearrange("p r w -> p (r w)")).then_inc(
                    s_mst[par * CH + c], 16)

            for l in range(NLAYER):
                if l == 0:
                    units(0, 0, 0)
                    def rows(b):
                        for s, (dst, src) in enumerate(((g[:, :, 0:C], ent_v), (z[:, :, :], x_v))):
                            sp.dma_start(dst, src[b]).then_inc(s_pin[s], 16)

                    rows(0)
                    with sp.Fori(1, NB) as b:
                        sp.wait_ge(s_ptr, 2 * b)
                        rows(b)
                    sp.wait_ge(s_uvst, 16 * 2 * NB)
                else:
                    sp.wait_ge(s_z, pair(l, 0, 0))
                    if l == 1:
                        for i in range(2 * CH):
                            sp.wait_ge(s_mst[i], 16 * NB // 2)
                    units(l, 0, 0)
                    sp.wait_ge(s_uvst, 16 * (2 * NB + NB * l))
                    sp.wait_ge(s_x1, 16 * NB * l)
                sp.dma_start(vw[:, :], uv_d[l, 0:1, :].broadcast_to([P, N])).then_inc(s_vb, 16)
                ub_load(l, 0, 0)

                def body(b, par, head, tail):
                    if tail:
                        xin_free(l, b - 1)
                        xin_load(l, b - 1)
                    if head:
                        first = isinstance(b, int) and b == 0
                        if l > 0 and not first:
                            sp.wait_ge(s_z, pair(l, b, 0))
                        units(l, b + 1, 1 - par)
                        if not (l == 0 and first):
                            sp.wait_ge(s_lr, pair(l, b, 0))
                        ub_load(l, b + 1, 1 - par)

                blocks(sp, body)
                xin_free(l, NB - 1)
                xin_load(l, NB - 1)
            for i in range(2 * CH):
                sp.wait_ge(s_mst[i], 16 * NB // 2)
            sp.wait_ge(s_uvst, 16 * 4 * NB)
            sp.wait_ge(s_x1, 16 * 2 * NB)
            sp.wait_ge(s_out, 16 * NB)

        @block.gpsimd
        def _(pool):
            for n, (m, v) in enumerate((
                    (wcat[:, :, :], 0.0), (wt[:, :, :], 0.0), (lbx[:, :, :], 0.0), (attc[:, :, :], 0.0),
                    (half[:, :], -0.5), (ones[:, :], 1.0), (ones3[:, :], 1.0), (ht[C:CE, :], 1.0),
                    (feat[:, :, :, C:CE], 1.0), (identb[:, :], 0.0), (nbig[:, :], 0.0), (ident[:, :], 0.0))):
                nc.gpsimd.memset(m, v).then_inc(s_zero, 1)
                pool.wait_ge(s_zero, n + 1)
            for m, v in ((ident, 1.0), (identb, 1.0), (nbig, -BIG)):
                nc.gpsimd.affine_select(out=m[:, :], in_=m[:, :], compare_op=ALU.not_equal, fill=v, base=0,
                                        pattern=[[-1, P]], channel_multiplier=1).then_inc(s_const, 1)
            with pool.Fori(0, NB) as b:
                for s in range(2):
                    pool.wait_ge(s_pout, 2 * b + s + 1)
                    nc.gpsimd.dma_start(uv_d[0, s:s + 1, bass.ds(b * BI, BI)], score[0:1, 0, s, :]).then_inc(s_uvst, 16)

            def tail(l, b):
                if l == 0:
                    pool.wait_ge(s_mom, blk(l, b) + 1)
                    nc.gpsimd.tensor_tensor(rstd[:, :], mom2[:, :], half[:, :], ALU.pow).then_inc(s_rstd, 1)
                if l < 2:
                    pool.wait_ge(s_oe, 4 * blk(l, b) + 4)
                    nc.gpsimd.dma_start(uv_d[l + 1, :, bass.ds(b * BI, BI)], uvrow[:, :]).then_inc(s_uvst, 16)
                    pool.wait_ge(s_y, blk(l, b) + 1)
                    nc.gpsimd.dma_start(xy_v[l, b], xin[:, :, :]).then_inc(s_x1, 16)
                else:
                    pool.wait_ge(s_mom2, b + 1)
                    nc.gpsimd.tensor_tensor(rstd[:, :], mom2[:, :], half[:, :], ALU.pow).then_inc(s_rstd2, 1)
                    pool.wait_ge(s_fin, b + 1)
                    nc.gpsimd.dma_start(out_v[b], pj[:, :, :]).then_inc(s_out, 16)

            for l in range(NLAYER):
                with pool.Fori(0, NB) as b:
                    tail(l, b)

        @block.scalar
        def _(act):
            for l in range(NLAYER):
                act.wait_ge(s_wt, l + 1)
                nc.scalar.activation(wt[:, l, 0:C], miscA[0:C, 0:C], ACT.Copy).then_inc(s_wte, 1)
            for l in range(NLAYER):
                act.wait_ge(s_wuv, l + 1)
                dst = wuv0[:, :] if l == 0 else wcat[:, l - 1, C:C + 2]
                nc.scalar.activation(dst, miscA[0:CE, 0:2], ACT.Copy).then_inc(s_wcat, 1)
            def first_scores(b):
                for s in range(2):
                    act.wait_ge(s_ptr, 2 * b + s + 1)
                    nc.scalar.activation(ht[0:C, :], miscA[0:C, :], ACT.Copy).then_inc(s_pte, 1)
                    act.wait_ge(s_pmm, 2 * b + s + 1)
                    if s == 0:
                        nc.scalar.activation(v8col[:, 0, bass.ds(b * RT, RT)], miscA[:, 0:RT], ACT.Copy,
                                             scale=1.0 - ALPHA)
                        nc.scalar.activation(v2col[:, 0, bass.ds(b * RT, RT)], miscA[:, 0:RT], ACT.Copy,
                                             scale=ALPHA)
                    else:
                        nc.scalar.activation(ucol[:, 0, bass.ds(b * RT, RT)], miscA[:, 0:RT], ACT.Copy)
                    if not (isinstance(b, int) and b == 0):
                        act.wait_ge(s_uvst, 32 * b)
                    nc.scalar.activation(score[0:1, 0, s, :], miscB[0:1, :], ACT.Copy).then_inc(s_pout, 1)

            first_scores(0)
            with act.Fori(1, NB) as b:
                first_scores(b)

            def leaky(l, b, t, par):
                g_ = pair(l, b, t)
                if not (l == 0 and isinstance(b, int) and b == 0 and t < TS):
                    act.wait_ge(s_main, g_ - TS + 1)
                if t == 0:
                    act.wait_ge(s_ub[par], ub_count(l, b, par))
                for jj in range(2):
                    j = 2 * t + jj
                    ins = nc.scalar.activation(score[:, t % TS, jj, :], ub[:, par, :], ACT.Relu,
                                               bias=v8col[:, l % 2, j:j + 1], scale=1.0 - ALPHA)
                ins.then_inc(s_lr, 1)

            def ub_count(l, b, par):
                return 16 * (l * (NB // 2)) + (16 * ((b - par) // 2 + 1) if isinstance(b, int) else
                                               8 * (b - par) + 16)

            def probs(l, b, t):
                act.wait_ge(s_add, pair(l, b, t) + 1)
                for jj in range(2):
                    j = 2 * t + jj
                    sc = score[:, t % TS, jj, :]
                    ins = nc.scalar.activation(sc, sc, ACT.Exp, bias=v2col[:, l % 2, j:j + 1])
                ins.then_inc(s_p, 1)

            def sums_out(l, b, par):
                act.wait_ge(s_main, pair(l, b, PAIRS))
                nc.scalar.activation(acc_s[:, :], acc[0:CE, par, :], ACT.Copy).then_inc(s_acce, 1)

            def tail_exp(l, b):
                act.wait_ge(s_ga, blk(l, b) + 1)
                nc.scalar.activation(e[:, :, :], e[:, :, :], ACT.Exp).then_inc(s_ex, 1)

            def columns_out(l, b):
                act.wait_ge(s_htt, blk(l, b) + 1)
                nc.scalar.activation(ht[0:C, :], miscA[0:C, :], ACT.Copy).then_inc(s_hte, 1)

            def products_out(l, b, i):
                n = 4 * blk(l, b) + i + 1
                act.wait_ge(s_om, n)
                if i < 2:
                    v = miscB[:, 0:2 * WC].rearrange("p (r w) -> p r w", w=WC)
                    if l < 2:
                        d = (l + 1) % 2
                        nc.scalar.activation(feat[:, d, bass.ds(b * RT + 2 * i, 2), 0:C], v[:, :, 0:C], ACT.Copy)
                        nc.scalar.activation(v8col[:, d, bass.ds(b * RT + 2 * i, 2)], v[:, :, C], ACT.Copy,
                                             scale=1.0 - ALPHA)
                        nc.scalar.activation(v2col[:, d, bass.ds(b * RT + 2 * i, 2)], v[:, :, C], ACT.Copy,
                                             scale=ALPHA)
                        nc.scalar.activation(ucol[:, d, bass.ds(b * RT + 2 * i, 2)], v[:, :, C + 1], ACT.Copy)
                    if i == 0:
                        if l == 2 and not (isinstance(b, int) and b == 0):
                            act.wait_ge(s_out, 16 * b)
                        elif not (isinstance(b, int) and b == 0 and l == 0):
                            act.wait_ge(s_y, blk(l, b))
                    nc.scalar.activation(pj[:, 2 * i:2 * i + 2, :], v[:, :, C + 2:WC], ACT.Copy).then_inc(
                        s_oe, 3 if l == 2 and i == 1 else 1)
                elif l < 2:
                    act.wait_ge(s_uvst, 16 * (2 * NB + blk(l, b)))
                    nc.scalar.activation(uvrow[:, :], miscB[0:2, :], ACT.Copy).then_inc(s_oe, 2)

            def maxima_out(l, b, par):
                act.wait_ge(s_mt, blk(l, b) + 1)
                nc.scalar.activation(mrow[:, par, :], miscAb[0:3, 0:BI], ACT.Copy).then_inc(s_mte, 1)

            def tail_step(l, b, par, t):
                if t == T_EVAC:
                    sums_out(l, b, par)
                if t == T_EXP:
                    tail_exp(l, b)
                if t == T_HTE:
                    columns_out(l, b)
                for i in range(3 if l < 2 else 2):
                    if t == T_OUTE + i:
                        products_out(l, b, i)

            for l in range(NLAYER):
                act.wait_ge(s_fsum, l + 1)
                nc.scalar.activation(fsum[:, :], miscB[:, 0:CE], ACT.Copy).then_inc(s_fsume, 1)
                maxima_out(l, 0, 0)
                leaky(l, 0, 0, 0)

                def body(b, par, head, tail):
                    for t in range(PAIRS):
                        if t > 0:
                            probs(l, b, t - 1)
                        elif tail:
                            probs(l, b - 1, PAIRS - 1)
                        if tail:
                            tail_step(l, b - 1, 1 - par, t)
                        if head and t == T_HEADT:
                            maxima_out(l, b + 1, 1 - par)
                        if t + 1 < PAIRS:
                            leaky(l, b, t + 1, par)
                        elif head:
                            leaky(l, b + 1, 0, 1 - par)

                blocks(act, body)
                probs(l, NB - 1, PAIRS - 1)
                for t in range(PAIRS):
                    tail_step(l, NB - 1, 1, t)

        @block.tensor
        def _(pe):
            pe.wait_ge(s_const, 3)
            pe.wait_ge(s_w, 16 * 14)
            pe.wait_ge(s_setup, SEQ_SETUP)
            for l in range(NLAYER):
                if l:
                    pe.wait_ge(s_wte, l)
                nc.tensor.transpose(miscA[0:C, 0:C], wld[:, l, :], ident[0:C, 0:C]).then_inc(s_wt, 1)
            pe.wait_ge(s_wte, NLAYER)
            for l in range(NLAYER):
                if l:
                    pe.wait_ge(s_wcat, l)
                mm = nc.tensor.matmul(miscA[0:CE, 0:2], wt[:, l, :], q[:, l, :], start=True, stop=(l == 0))
                if l:
                    mm = nc.tensor.matmul(miscA[0:CE, 0:2], lbx[:, l - 1, :], attc[:, l - 1, :], start=False,
                                          stop=True)
                mm.then_inc(s_wuv, 1)
            pe.wait_ge(s_wcat, NLAYER)
            for b in range(NB):
                for s in range(2):
                    src = g if s == 0 else z
                    if b or s:
                        pe.wait_ge(s_pout, 2 * b + s)
                    pe.wait_ge(s_pin[s], 16 * b + 16)
                    for r in range(RT):
                        mm = nc.tensor.transpose(miscA[0:C, r * P:(r + 1) * P], src[:, r, 0:C], ident[:, :])
                    mm.then_inc(s_ptr, 1)
                    pe.wait_ge(s_pte, 2 * b + s + 1)
                    for r in range(RT):
                        nc.tensor.matmul(miscA[:, r:r + 1], ht[:, r * P:(r + 1) * P], wuv0[:, s:s + 1],
                                         start=True, stop=True)
                    nc.tensor.matmul(miscB[0:1, :], wuv0[:, s:s + 1], ht[:, :], start=True,
                                     stop=True).then_inc(s_pmm, 1)

            def build_z(l, b, t, par):
                g_ = pair(l, b, t)
                if not (l == 0 and isinstance(b, int) and b == 0 and t < ZS):
                    pe.wait_ge(s_add, g_ - ZS + 1)
                if t == 0:
                    pe.wait_ge(s_mte, blk(l, b) + 1)
                for jj in range(2):
                    j = 2 * t + jj
                    zt = zps[:, t % ZS, jj, :]
                    c, o = divmod(j * P, CW)
                    nc.tensor.matmul(zt, ones3[:, :], mrow[:, par, :], start=True, stop=False)
                    for r in range(RT):
                        mm = nc.tensor.matmul(zt[:, r * P:(r + 1) * P], mask[:, par, c, r, o:o + P].bitcast(FP8), nbig[:, :],
                                              start=False, stop=(r == RT - 1))
                mm.then_inc(s_z, 1)

            def main(l, b, t, par):
                pe.wait_ge(s_p, pair(l, b, t) + 1)
                if t == 0:
                    if not (l == 0 and isinstance(b, int) and b < 2):
                        pe.wait_ge(s_acce, blk(l, b) - 1)
                for jj in range(2):
                    j = 2 * t + jj
                    mm = nc.tensor.matmul(acc[0:CE, par, :], feat[:, l % 2, j, :], score[:, t % TS, jj, :],
                                          start=(j == 0), stop=(j == NT - 1))
                mm.then_inc(s_main, 1)

            def turn_maxima(l, b):
                pe.wait_ge(s_split, blk(l, b) + 1)
                for r in range(RT):
                    mm = nc.tensor.transpose(miscAb[0:3, r * P:(r + 1) * P], parts[:, r, 0:3], identb[:, :])
                mm.then_inc(s_mt, 1)

            def tail_step(l, b, t):
                if t == T_TURN:
                    pe.wait_ge(s_acce, blk(l, b) + 1)
                    for r in range(RT):
                        mm = nc.tensor.transpose(miscA[:, r * CE:(r + 1) * CE], acc_s[:, r * P:(r + 1) * P],
                                                 ident[0:CE, 0:CE])
                    mm.then_inc(s_gt, 1)
                if t == T_HT:
                    for r in range(RT):
                        mm = nc.tensor.transpose(miscA[0:C, r * P:(r + 1) * P], hn[:, r, :], ident[:, :])
                    mm.then_inc(s_htt, 1)
                for i in range(2):
                    if t == T_OUT + i:
                        if i == 0:
                            pe.wait_ge(s_hte, blk(l, b) + 1)
                            if not (l == 0 and isinstance(b, int) and b == 0):
                                pe.wait_ge(s_oe, 4 * blk(l, b))
                        else:
                            pe.wait_ge(s_oe, 4 * blk(l, b) + 1)
                        for r in range(2):
                            mm = nc.tensor.matmul(miscB[:, r * WC:(r + 1) * WC],
                                                  ht[:, (2 * i + r) * P:(2 * i + r + 1) * P], wcat[:, l, :],
                                                  start=True, stop=True)
                        mm.then_inc(s_om, 3 if l == 2 and i == 1 else 1)
                if t == T_OUT + 2 and l < 2:
                    pe.wait_ge(s_oe, 4 * blk(l, b) + 2)
                    if True:
                        nc.tensor.matmul(miscB[0:2, :], wcat[:, l, C:C + 2], ht[:, :], start=True,
                                         stop=True).then_inc(s_om, 2)

            for l in range(NLAYER):
                if l == 0:
                    pe.wait_ge(s_feat0, 16)
                    pe.wait_ge(s_pout, 2 * NB)
                else:
                    pe.wait_ge(s_oe, 4 * blk(l, 0))
                for j in range(NT):
                    mm = nc.tensor.matmul(miscB[:, 0:CE], ones[:, :], feat[:, l % 2, j, :], start=(j == 0),
                                          stop=(j == NT - 1))
                mm.then_inc(s_fsum, 1)
                turn_maxima(l, 0)

                def body(b, par, head, tail):
                    for t in range(PAIRS):
                        if tail and t == T_HT:
                            pe.wait_ge(s_h, blk(l, b))
                        build_z(l, b, t, par)
                        if t >= 2:
                            main(l, b, t - 2, par)
                        elif tail:
                            main(l, b - 1, PAIRS - 2 + t, 1 - par)
                        if tail:
                            tail_step(l, b - 1, t)
                        if head and t == T_HEADT:
                            turn_maxima(l, b + 1)

                blocks(pe, body)
                main(l, NB - 1, PAIRS - 2, 1)
                main(l, NB - 1, PAIRS - 1, 1)
                for t in range(PAIRS):
                    if t == T_HT:
                        pe.wait_ge(s_h, blk(l, NB))
                    tail_step(l, NB - 1, t)

        @block.vector
        def _(dve):
            dv = nc.vector

            def step(ins, seq, n):
                ins.then_inc(seq, 1)
                dve.wait_ge(seq, n)

            dve.wait_ge(s_w, 16 * 14)
            for l in range(2):
                for s in range(2):
                    dv.tensor_tensor_reduce(out=acc_s[0:C, (2 * l + s) * HID:(2 * l + s + 1) * HID], in0=lin[:, l, s, :], in1=att[:, l, :], scale=1.0,
                                            scalar=0.0, op0=ALU.mult, op1=ALU.add,
                                            accum_out=q[:, l + 1, 1 - s:2 - s]).then_inc(s_setup, 1)

            def make_mask(b, par, u):
                c, r = divmod(u, RT)
                dve.wait_ge(s_stage[r], 16 * (b * CH + c + 1))
                if not (isinstance(b, int) and b < 2) and r == 0:
                    dve.wait_ge(s_mst[par * CH + c], 8 * (b - par))
                    dve.wait_ge(s_z, pair(0, b - 1, 0))
                dv.tensor_scalar(mask[:, par, c, r, :], stage[:, r, :], 0, ONE8, ALU.is_le, ALU.mult).then_inc(s_mask, 1)

            def unit_min(l, b, par, u):
                c, r = divmod(u, RT)
                if l > 0 and r == 0:
                    landed = 16 * ((b - par) // 2 + 1) if isinstance(b, int) else 8 * (b - par) + 16
                    dve.wait_ge(s_mload[par * CH + c], 16 * (l - 1) * (NB // 2) + landed)
                    dv.memset(st[:, 8 + c:9 + c], 0.0)
                dv.tensor_tensor_reduce(out=junk[:, u % 2, :], in0=mask[:, par, c, r, :], in1=vw[:, c * CW:(c + 1) * CW],
                                        scale=1.0, scalar=2.0, op0=ALU.add, op1=ALU.min,
                                        accum_out=pw[:, r, c:c + 1]).then_inc(s_unit, 1)

            def head(l, b, par):
                at = blk(l, b) * SEQ_HEAD
                dve.wait_ge(s_unit, (blk(l, b) + 1) * UNITS)
                step(dv.tensor_reduce(w4[:, :], pw[:, :, :], AX, ALU.min), s_headseq, at + 1)
                step(dv.tensor_scalar(emp[:, par, :], w4[:, :], 1.0, None, ALU.is_ge), s_headseq, at + 2)
                step(dv.scalar_tensor_tensor(ns[:, :], w4[:, :], st[:, 4:5], nuv[:, bass.ds(b * RT, RT)], ALU.mult,
                                             ALU.add), s_headseq, at + 3)
                step(dv.scalar_tensor_tensor(nm[:, :], ns[:, :], ALPHA, ns[:, :], ALU.mult, ALU.min),
                     s_headseq, at + 4)
                step(dv.scalar_tensor_tensor(nm[:, :], ucol[:, l % 2, bass.ds(b * RT, RT)], ALPHA, nm[:, :],
                                             ALU.mult, ALU.add), s_headseq, at + 5)
                if not (l == 0 and isinstance(b, int) and b == 0):
                    dve.wait_ge(s_mt, blk(l, b))
                step(dv.tensor_copy(parts[:, :, 0], nm[:, :]), s_headseq, at + 6)
                step(dv.tensor_tensor(r1[:, :], nm[:, :], parts[:, :, 0], ALU.subtract), s_headseq, at + 7)
                step(dv.tensor_copy(parts[:, :, 1], r1[:, :]), s_headseq, at + 8)
                step(dv.tensor_tensor(nm[:, :], r1[:, :], parts[:, :, 1], ALU.subtract), s_headseq, at + 9)
                dv.tensor_copy(parts[:, :, 2], nm[:, :]).then_inc(s_split, 1)

            def spread(a):
                return a.rearrange("p (r o) -> p r o", o=1).broadcast_to([P, RT, C])

            def row_sums_to_means(src, seq, at):
                step(dv.tensor_reduce(mom[:, :], src, AX, ALU.add), seq, at + 1)
                step(dv.tensor_scalar(mom[:, :], mom[:, :], 1.0 / C, None, ALU.mult), seq, at + 2)

            def variances(src):
                for r in range(RT):
                    ins = dv.tensor_tensor_reduce(out=z[:, r, :], in0=src[:, r, :], in1=src[:, r, :], scale=1.0 / C,
                                                  scalar=EPS, op0=ALU.mult, op1=ALU.add, accum_out=mom2[:, r:r + 1])
                return ins

            def tail_aggregate(l, b, par):
                seq, at = s_tailseq[l], b * SEQ_TAIL[l]
                dve.wait_ge(s_gt, blk(l, b) + 1)
                dve.wait_ge(s_fsume, l + 1)
                for r in range(RT):
                    ins = dv.scalar_tensor_tensor(g[:, r, :], fsum[:, :], emp[:, par, r:r + 1],
                                                  miscA[:, r * CE:(r + 1) * CE], ALU.mult, ALU.add)
                step(ins, seq, at + 1)
                step(dv.reciprocal(rden[:, :], g[:, :, C]), seq, at + 2)
                step(dv.tensor_tensor(z[:, :, :], g[:, :, 0:C], spread(rden[:, :]), ALU.mult), seq, at + 3)
                dve.wait_ge(s_xin, 16 * (blk(l, b) + 1))
                if l == 0:
                    step(dv.tensor_tensor(z[:, :, :], z[:, :, :], xin[:, :, 0:C], ALU.add), seq, at + 4)
                if not (l == 0 and isinstance(b, int) and b == 0):
                    dve.wait_ge(s_htt, blk(l, b))
                dv.tensor_scalar(hn[:, :, :], z[:, :, :], 0.0, -1.0, ALU.max, ALU.add)
                dv.tensor_scalar(e[:, :, :], z[:, :, :], 0.0, None, ALU.min).then_inc(s_ga, 1)

            def tail_features(l, b):
                seq, at = s_tailseq[l], b * SEQ_TAIL[l] + (4 if l == 0 else 3)
                dve.wait_ge(s_ex, blk(l, b) + 1)
                step(dv.tensor_tensor(hn[:, :, :], hn[:, :, :], e[:, :, :], ALU.add), seq, at + 1)
                if l == 0:
                    step(dv.tensor_tensor(hn[:, :, :], hn[:, :, :], xin[:, :, 0:C], ALU.add), seq, at + 2)
                    row_sums_to_means(hn[:, :, :], seq, at + 2)
                    step(dv.tensor_tensor(hn[:, :, :], hn[:, :, :], spread(mom[:, :]), ALU.subtract), seq, at + 5)
                    variances(hn).then_inc(s_mom, 1)
                else:
                    step(dv.tensor_scalar(z[:, :, :], xin[:, :, 0:C], ALPHA, None, ALU.mult), seq, at + 2)
                    dv.scalar_tensor_tensor(hn[:, :, :], hn[:, :, :], 1.0 - ALPHA, z[:, :, :], ALU.mult,
                                            ALU.add).then_inc(s_h, 1)

            def tail_norm(b):
                dve.wait_ge(s_rstd, b + 1)
                dv.tensor_tensor(hn[:, :, :], hn[:, :, :], spread(rstd[:, :]), ALU.mult).then_inc(s_h, 1)

            def tail_output(l, b):
                dve.wait_ge(s_oe, 4 * blk(l, b) + 2)
                yb = xin[:, :, C:2 * C]
                if l == 0:
                    dve.wait_ge(s_h, blk(l, b) + 1)
                    dv.tensor_copy(xin[:, :, 0:C], hn[:, :, :])
                    dv.tensor_tensor(yb, hn[:, :, :], pj[:, :, :], ALU.add).then_inc(s_y, 1)
                elif l == 1:
                    dv.tensor_tensor(yb, yb, pj[:, :, :], ALU.add).then_inc(s_y, 1)
                else:
                    seq, at = s_tailseq[l], b * SEQ_TAIL[l] + 5
                    step(dv.tensor_tensor(pj[:, :, :], yb, pj[:, :, :], ALU.add), seq, at + 1)
                    row_sums_to_means(pj[:, :, :], seq, at + 1)
                    step(dv.tensor_tensor(pj[:, :, :], pj[:, :, :], spread(mom[:, :]), ALU.subtract), seq, at + 4)
                    variances(pj).then_inc(s_mom2, 1)

            def tail_result(b):
                dve.wait_ge(s_rstd2, b + 1)
                dv.tensor_tensor(pj[:, :, :], pj[:, :, :], spread(rstd[:, :]), ALU.mult).then_inc(s_fin, 1)

            def tail_step(l, b, par, t):
                if t == T_A:
                    tail_aggregate(l, b, par)
                if t == T_B:
                    tail_features(l, b)
                if t == T_C and l == 0:
                    tail_norm(b)
                if t == T_Y:
                    tail_output(l, b)
                if t == T_D and l == 2:
                    tail_result(b)

            def add(l, b, t):
                dve.wait_ge(s_z, pair(l, b, t) + 1)
                dve.wait_ge(s_lr, pair(l, b, t) + 1)
                sc = score[:, t % TS, :, :]
                dv.tensor_tensor(sc, sc, zps[:, t % ZS, :, :], ALU.add).then_inc(s_add, 1)

            for l in range(NLAYER):
                if l == 0:
                    for u in range(UNITS):
                        make_mask(0, 0, u)
                at = SEQ_START * l
                dve.wait_ge(s_vb, 16 * (l + 1))
                step(dv.tensor_reduce(st[:, 0:1], vw[:, :], AX, ALU.max), s_startseq, at + 1)
                step(dv.tensor_reduce(st[:, 1:2], vw[:, :], AX, ALU.min), s_startseq, at + 2)
                step(dv.tensor_tensor(st[:, 2:3], st[:, 1:2], st[:, 0:1], ALU.subtract), s_startseq, at + 3)
                step(dv.tensor_scalar(st[:, 2:3], st[:, 2:3], 1.001, -1e-30, ALU.mult, ALU.add), s_startseq, at + 4)
                step(dv.reciprocal(st[:, 3:4], st[:, 2:3]), s_startseq, at + 5)
                step(dv.tensor_scalar(st[:, 4:5], st[:, 2:3], -1.0, None, ALU.mult), s_startseq, at + 6)
                step(dv.tensor_scalar(vw[:, :], vw[:, :], st[:, 0:1], st[:, 3:4], ALU.subtract, ALU.mult),
                     s_startseq, at + 7)
                if l == 0:
                    dve.wait_ge(s_pout, 2 * NB)
                else:
                    dve.wait_ge(s_oe, 4 * blk(l, 0))
                step(dv.tensor_scalar(nuv[:, :], ucol[:, l % 2, :], st[:, 0:1], -1.0, ALU.add, ALU.mult),
                     s_startseq, at + 8)
                if l == 0:
                    dve.wait_ge(s_mask, UNITS)
                for u in range(UNITS):
                    if l * NB * UNITS + u > 1:
                        dve.wait_ge(s_unit, blk(l, 0) * UNITS + u - 1)
                    unit_min(l, 0, 0, u)
                head(l, 0, 0)

                def body(b, par, head_, tail_):
                    for t in range(PAIRS):
                        for u in (UNIT_AT_0 if l == 0 else UNIT_AT).get(t, []) if head_ else []:
                            dve.wait_ge(s_unit, blk(l, b + 1) * UNITS + u - 1)
                        add(l, b, t)
                        if tail_:
                            tail_step(l, b - 1, 1 - par, t)
                        if head_:
                            if l == 0:
                                for u in range(UNITS + 1):
                                    if t == u * T_UNITS // UNITS:
                                        if u > 0:
                                            dve.wait_ge(s_mask, (b + 1) * UNITS + u)
                                        if u < UNITS:
                                            make_mask(b + 1, 1 - par, u)
                                        else:
                                            dv.memset(st[:, 8:9], 0.0)
                                        if u > 0:
                                            unit_min(l, b + 1, 1 - par, u - 1)
                            else:
                                for u in UNIT_AT.get(t, []):
                                    unit_min(l, b + 1, 1 - par, u)
                            if t == T_HEAD:
                                head(l, b + 1, 1 - par)

                blocks(dve, body)
                for t in range(PAIRS):
                    tail_step(l, NB - 1, 1, t)


_INS = ["x", "adj", "L0_gnn_entity_embs", "L0_gnn_W", "L0_gnn_a", "L1_gnn_W", "L1_gnn_lin_w", "L1_gnn_lin_b",
        "L1_gnn_attn", "L1_gnn_mlp_w", "L1_gnn_mlp_b"]


def kernel(**inputs):
    import numpy as _np
    import concourse.bacc as _bacc
    from concourse import mybir as _mybir
    from concourse.bass_utils import run_bass_kernel_spmd as _run

    nc = _bacc.Bacc("TRN2", target_bir_lowering=False, num_devices=1)
    arrays, args = {}, []
    for name in _INS:
        a = _np.ascontiguousarray(inputs[name])
        arrays[f"in_{name}_dram"] = a
        args.append(nc.dram_tensor(f"in_{name}_dram", a.shape, _mybir.dt.from_np(a.dtype), kind="ExternalInput").ap())
    args.append(nc.dram_tensor("out_0_dram", (N, C), F32, kind="ExternalOutput").ap())
    build(nc, *args)
    r = _run(nc, [arrays], core_ids=[0])
    return r.results[0]["out_0_dram"]
```

```python
from contextlib import ExitStack

import concourse.bass as bass
from concourse import mybir

ALU = mybir.AluOpType
ACT = mybir.ActivationFunctionType
F32 = mybir.dt.float32
BF16 = mybir.dt.bfloat16
FP8 = mybir.dt.float8e4
I32 = mybir.dt.int32
U8 = mybir.dt.uint8
ONE8 = 56
AX = mybir.AxisListType.X

P = 128
N = 8192
C = 64
HID = 32
CE = C + 1
NT = N // P
BI = 512
RT = BI // P
NB = N // BI
CH = 8
CW = N // CH
UNITS = CH * RT
MV = 4
V_AT = 12
SS = 8
NLAYER = 3
ALPHA = 0.2
BIG = 9.0e15
EPS = 1e-5
TS = 4
ES = 5
AHEAD = 3
LAG = 3
ACT_TILES = ((1, 2, 4, 5, 6), (2, 4, 6), (2, 4, 6))
ON_ACT = tuple(frozenset(j for j in range(AHEAD, NT) if j % 7 in ks) for ks in ACT_TILES)
WC = 2 * C + 2

SEQ_SETUP = 4
SEQ_PREP = 4
SEQ_START = 10
SEQ_HEAD = 9
SEQ_TAIL = (9, 5, 9)

T_EVAC = 6
T_TURN = 8
T_A = 10
T_EXP = 14
T_B = 17
T_C = 20
T_HT = 24
T_HTE = 26
T_OUT = 28
T_OUTE = 30
T_Y = 35
T_D = 39
T_UNITS = 56
T_HEAD = 56
T_HEADT = 59
T_ROWS = 60
T_UA = 62


def unit_slots():
    at = {}
    for u in range(UNITS):
        at.setdefault(u * T_UNITS // UNITS, []).append(u)
    return at


UNIT_AT = unit_slots()
UNIT_AT_0 = {(u + 1) * T_UNITS // UNITS: [u] for u in range(UNITS)}


def build(nc, x, adj, ent, W0, a0, W12, lin_w, lin_b, attn, mlp_w, mlp_b, out):
    with ExitStack() as ctx:
        def sb(name, shape, dt=F32):
            return ctx.enter_context(nc.sbuf_tensor(name, shape, dt))

        def ps(name, shape, dt=F32):
            return ctx.enter_context(nc.psum_tensor(name, shape, dt))

        def sem(name):
            return ctx.enter_context(nc.semaphore(name))

        mask_d = [nc.dram_tensor(f"mask_d{m}", [NB, P, RT * N // MV], U8).ap() for m in range(MV)]
        uv_d = nc.dram_tensor("uv_d", [NLAYER, 2, N], F32).ap()
        xy_d = nc.dram_tensor("xy_d", [2, N, 2 * C], F32).ap()

        mask = sb("mask", [P, 2, CH, RT, CW], U8)
        stage = sb("stage", [P, SS, CW], I32)
        vw = sb("vw", [P, N])
        feat = sb("feat", [P, 2, NT, CE])
        prob = sb("prob", [P, TS, BI])
        ub = sb("ub", [P, 2, BI])
        cb = sb("cb", [P, 2, BI])
        ua = sb("ua", [P, 2, BI])
        xin = sb("xin", [P, RT, 2 * C])
        acc_s = sb("acc_s", [CE, BI])
        g = sb("g", [P, RT, CE])
        z = sb("z", [P, RT, C])
        e = sb("e", [P, RT, C])
        hn = sb("hn", [P, RT, C])
        ht = sb("ht", [CE, BI])
        uvrow = sb("uvrow", [2 * RT, P])
        uvrow0 = z[0:NT, :, :].rearrange("t r c -> t (r c)").rearrange("t (s p) -> t s p", s=2)
        vu = sb("vu", [P, 2, RT])
        pj = sb("pj", [P, RT, C])
        v8col = sb("v8col", [P, NT])
        v2col = sb("v2col", [P, NT])
        vucol = sb("vucol", [P, 2, 2, NT])
        nuv = sb("nuv", [P, NT])
        st = sb("st", [P, 16])
        fsum = sb("fsum", [P, CE])
        pw = sb("pw", [P, RT, CH])
        w4 = sb("w4", [P, RT])
        ns = sb("ns", [P, RT])
        nm = sb("nm", [P, RT])
        r1 = sb("r1", [P, RT])
        emp = sb("emp", [P, 2, RT])
        parts = sb("parts", [P, RT, 4], BF16)
        mrow = sb("mrow", [3, 2, BI], BF16)
        rden = sb("rden", [P, RT])
        mom = sb("mom", [P, RT])
        mom2 = sb("mom2", [P, RT])
        half = sb("half", [P, RT])
        rstd = sb("rstd", [P, RT])
        wcat = sb("wcat", [CE, NLAYER, WC])
        w0row = sb("w0row", [P, 2, C])
        q0 = e[0:C, :, :].rearrange("f r c -> f (r c)").rearrange("f (s p) -> f s p", s=2)
        wt = sb("wt", [C, NLAYER, CE])
        q = sb("q", [C, NLAYER, 2])
        lin = sb("lin", [C, 2, 2, HID])
        att = sb("att", [C, 2, HID])
        lbx = sb("lbx", [HID, 2, CE])
        attc = sb("attc", [HID, 2, 2])
        wld = xin[0:C, 0:NLAYER, 0:C]
        junk = sb("junk", [P, 2, CW], U8)
        ident = sb("ident", [P, P])
        identb = sb("identb", [P, P], BF16)
        nbig = sb("nbig", [P, P], BF16)
        ones = sb("ones", [P, P])
        ones3 = sb("ones3", [3, P], BF16)

        eps = ps("eps", [P, ES, BI])
        acc = ps("acc", [P, 2, BI])
        misc = ps("misc", [P, BI])
        miscb = misc[:, :].bitcast(BF16)

        s_w = sem("weights_landed")
        s_zero = sem("memsets_done")
        s_const = sem("constants_done")
        s_wt = sem("w_turned")
        s_wte = sem("w_turned_out")
        s_wuv = sem("wuv_done")
        s_wcat = sem("wcat_done")
        s_x0 = sem("x_landed")
        s_q0 = sem("a_spread")
        s_w0 = sem("w0row_done")
        s_w0e = sem("w0row_out")
        s_prep = sem("prep_steps")
        s_pt = sem("prep_turned")
        s_pte = sem("prep_turned_out")
        s_feat0 = sem("entity_features_landed")
        s_vb = sem("v_rows_landed")
        s_v0 = sem("first_v_stored")
        s_uvst = sem("uv_rows_stored")
        s_fsum = sem("feature_sum_done")
        s_fsume = sem("feature_sum_out")
        s_start = sem("layer_start_done")
        s_stage = [sem(f"adjacency_landed{i}") for i in range(SS)]
        s_mask = sem("mask_unit_made")
        s_unit = sem("unit_minimum_done")
        s_mload = [sem(f"mask_loaded{i}") for i in range(2 * MV)]
        s_mst = [sem(f"mask_stored{i}") for i in range(2 * MV)]
        s_ub = [sem("ub_landed0"), sem("ub_landed1")]
        s_xin = sem("xin_landed")
        s_prime = sem("banks_primed")
        s_fill = sem("scores_started_by_dve")
        s_filla = sem("scores_started_by_act")
        s_z = sem("scores_masked")
        s_p = sem("probs_done")
        s_main = sem("probs_used")
        s_setup = sem("setup_steps")
        s_startseq = sem("layer_start_steps")
        s_headseq = sem("head_steps")
        s_tailseq = [sem(f"tail_steps{l}") for l in range(NLAYER)]
        s_split = sem("maxima_split")
        s_mt = sem("maxima_turned")
        s_mte = sem("maxima_rows_out")
        s_cb = sem("maxima_spread")
        s_cbe = sem("maxima_spread_out")
        s_ua = sem("ua_done")
        s_acce = sem("sums_out")
        s_gt = sem("sums_turned")
        s_ga = sem("tail_a_done")
        s_ex = sem("tail_exp_done")
        s_mom = sem("variance_done")
        s_rstd = sem("rstd_done")
        s_h = sem("features_done")
        s_htt = sem("features_turned")
        s_hte = sem("features_columns_out")
        s_om = sem("next_products")
        s_oe = sem("next_products_out")
        s_y = sem("output_sums_done")
        s_x1 = sem("x1_stored")
        s_mom2 = sem("last_variance_done")
        s_rstd2 = sem("last_rstd_done")
        s_fin = sem("result_done")
        s_out = sem("result_stored")

        def blk(l, b):
            return l * NB + b

        def tile(l, b, j):
            return (l * NB + b) * NT + j

        def freed(l, b, j):
            if j >= ES:
                return tile(l, b, j) - ES + 1
            last = max(i for i in range(NT) if i % ES == j)
            return tile(l, b, last) - NT + 1

        def started(l, b, j, on_act):
            def some(k, n):
                return sum((i in ON_ACT[k]) == on_act for i in range(n))
            return NB * sum(some(k, NT) for k in range(l)) + b * some(l, NT) + some(l, j + 1)

        def ub_count(l, b, par):
            in_layer = 16 * ((b - par) // 2 + 1) if isinstance(b, int) else 8 * (b - par) + 16
            return 16 * l * (NB // 2) + in_layer

        def blocks(eng, body):
            body(0, 0, True, False)
            body(1, 1, True, True)
            body(2, 0, True, True)
            with eng.Fori(0, (NB - 4) // 2) as k:
                body(2 * k + 3, 1, True, True)
                body(2 * k + 4, 0, True, True)
            body(NB - 1, 1, False, True)

        adj_v = adj.rearrange("(b r p) (c w) -> b c r p w", r=RT, p=P, w=CW)
        x_v = x.rearrange("(b r p) c -> b p r c", r=RT, p=P)
        ent_v = ent.rearrange("(b r p) c -> b p r c", r=RT, p=P)
        xy_v = xy_d.rearrange("l (b r p) c -> l b p r c", r=RT, p=P)
        out_v = out.rearrange("(b r p) c -> b p r c", r=RT, p=P)

        block = ctx.enter_context(nc.Block())

        @block.sync
        def _(sp):
            n_w = 0

            def w_load(dst, src):
                sp.dma_start(dst, src).then_inc(s_w, 16)

            sp.wait_ge(s_zero, 4)
            w_load(wld[:, 0, :], W0)
            w_load(wld[:, 1:3, :], W12.rearrange("l f g -> f l g"))
            w_load(wcat[0:C, 0:2, 0:C], W12.rearrange("l f g -> f l g"))
            w_load(wcat[0:C, :, C + 2:WC], mlp_w.rearrange("(l f) g -> f l g", l=NLAYER))
            w_load(wcat[C:CE, 0, C + 2:WC], mlp_b.rearrange("(o g) -> o g", o=1))
            with nc.allow_non_contiguous_dma(reason="a few hundred weights"):
                w_load(q[:, 0, 0:1], a0[C:2 * C, :])
                w_load(q[:, 0, 1:2], a0[0:C, :])
                w_load(lin[:, :, :, :], lin_w.rearrange("l (s f) h -> f l s h", s=2))
                for l in range(2):
                    w_load(att[:, l, :], attn[l].rearrange("h o -> o h").broadcast_to([C, HID]))
                    w_load(lbx[:, l, C:CE], lin_b[l].rearrange("(h o) -> h o", o=1))
                    w_load(attc[:, l, 1:2], attn[l])
            sp.dma_start(feat[:, 0, :, 0:C], ent.rearrange("(t p) c -> p t c", p=P)).then_inc(s_feat0, 16)

            def ub_load(l, b, par):
                if not (l == 0 and isinstance(b, int) and b < 2):
                    sp.wait_ge(s_z, tile(l, b - 1, 0))
                sp.dma_start(ub[:, par, :], uv_d[l, 1:2, bass.ds(b * BI, BI)].broadcast_to([P, BI])).then_inc(
                    s_ub[par], 16)

            def xin_load(l, b):
                if l == 0:
                    sp.dma_start(xin[:, :, 0:C], x_v[b]).then_inc(s_xin, 16)
                else:
                    sp.dma_start(xin[:, :, :], xy_v[l - 1, b]).then_inc(s_xin, 16)

            def xin_free(l, b):
                if isinstance(b, int) and b == 0 and l != 1:
                    return
                if l < 2:
                    sp.wait_ge(s_x1, 16 * blk(l, b))
                else:
                    sp.wait_ge(s_mom2, b)

            def v_load(l):
                sp.dma_start(vw[:, :], uv_d[l, 0:1, :].broadcast_to([P, N])).then_inc(s_vb, 16)

            def units(l, b, par):
                if not isinstance(b, int):
                    sp.compute_val(b * (P * RT * N // MV))
                for u in range(UNITS):
                    if u == SS and l == 0 and not (isinstance(b, int) and b == 0):
                        ub_load(l, b, par)
                    elif u == SS and l == 0:
                        sp.dma_start(feat[:, 1, :, 0:C], x.rearrange("(t p) c -> p t c", p=P)).then_inc(s_x0, 16)
                    elif u == V_AT and l == 0 and isinstance(b, int) and b == 0:
                        sp.wait_ge(s_v0, 16)
                        v_load(0)
                    c, r = divmod(u, RT)
                    if l == 0:
                        if not (isinstance(b, int) and b == 0 and u < SS):
                            sp.wait_ge(s_mask, blk(0, b) * UNITS + u - SS + 1)
                        sp.dma_start(stage[:, u % SS, :], adj_v[b, c, r]).then_inc(s_stage[u % SS], 16)
                        m, o = divmod(u + 1 - RT, UNITS // MV)
                        if m > 0 and o == 0:
                            store(b, m - 1, par)
                    elif u % (UNITS // MV) == 0:
                        m = u // (UNITS // MV)
                        if not (isinstance(b, int) and b < 2):
                            sp.wait_ge(s_z, tile(l, b - 2, (m + 1) * NT // MV))
                        sp.dma_start(moved(par, m), mask_d[m][b]).then_inc(s_mload[par * MV + m], 16)
                if l == 0:
                    store(b, MV - 1, par)

            def moved(par, m):
                w = CH // MV
                return mask[:, par, m * w:(m + 1) * w, :, :].rearrange("p c r w -> p (c r w)")

            def store(b, m, par):
                sp.wait_ge(s_mask, (b * MV + m + 1) * (UNITS // MV))
                sp.dma_start(mask_d[m][b], moved(par, m)).then_inc(s_mst[par * MV + m], 16)

            for l in range(NLAYER):
                if l == 0:
                    units(0, 0, 0)
                    sp.wait_ge(s_uvst, 16)
                else:
                    sp.wait_ge(s_z, tile(l, 0, 0))
                    if l == 1:
                        for i in range(2 * MV):
                            sp.wait_ge(s_mst[i], 16 * NB // 2)
                    units(l, 0, 0)
                    sp.wait_ge(s_uvst, 16 + 32 * NB * l)
                    v_load(l)
                    sp.wait_ge(s_x1, 16 * NB * l)
                ub_load(l, 0, 0)

                def body(b, par, head, tail):
                    if tail:
                        xin_free(l, b - 1)
                        xin_load(l, b - 1)
                    if head:
                        units(l, b + 1, 1 - par)
                        if l > 0:
                            ub_load(l, b + 1, 1 - par)

                blocks(sp, body)
                xin_free(l, NB - 1)
                xin_load(l, NB - 1)
            for i in range(2 * MV):
                sp.wait_ge(s_mst[i], 16 * NB // 2)
            sp.wait_ge(s_uvst, 16 + 32 * 2 * NB)
            sp.wait_ge(s_x1, 16 * 2 * NB)
            sp.wait_ge(s_out, 16 * NB)

        @block.gpsimd
        def _(pool):
            for n, (m, v) in enumerate((
                    (wcat[:, :, :], 0.0), (wt[:, :, :], 0.0), (lbx[:, :, :], 0.0), (attc[:, :, :], 0.0),
                    (half[:, :], -0.5), (ones[:, :], 1.0), (ones3[:, :], 1.0), (ht[C:CE, :], 1.0),
                    (feat[:, :, :, C:CE], 1.0), (identb[:, :], 0.0), (nbig[:, :], 0.0), (ident[:, :], 0.0))):
                nc.gpsimd.memset(m, v).then_inc(s_zero, 1)
                pool.wait_ge(s_zero, n + 1)
            for m, v in ((ident, 1.0), (identb, 1.0), (nbig, -BIG)):
                nc.gpsimd.affine_select(out=m[:, :], in_=m[:, :], compare_op=ALU.not_equal, fill=v, base=0,
                                        pattern=[[-1, P]], channel_multiplier=1).then_inc(s_const, 1)
            for s in range(2):
                pool.wait_ge(s_pte, s + 1)
                nc.gpsimd.dma_start(uv_d[0, s].rearrange("(t p) -> t p", p=P), uvrow0[:, s, :]).then_inc(
                    s_uvst if s else s_v0, 16)

            def tail(l, b):
                if l == 0:
                    pool.wait_ge(s_mom, blk(l, b) + 1)
                    nc.gpsimd.tensor_tensor(rstd[:, :], mom2[:, :], half[:, :], ALU.pow).then_inc(s_rstd, 1)
                if l < 2:
                    pool.wait_ge(s_oe, 4 * blk(l, b) + 4)
                    for s in range(2):
                        nc.gpsimd.dma_start(
                            uv_d[l + 1, s, bass.ds(b * BI, BI)].rearrange("(r p) -> r p", p=P),
                            uvrow[s * RT:(s + 1) * RT, :]).then_inc(s_uvst, 16)
                    pool.wait_ge(s_y, blk(l, b) + 1)
                    nc.gpsimd.dma_start(xy_v[l, b], xin[:, :, :]).then_inc(s_x1, 16)
                else:
                    pool.wait_ge(s_mom2, b + 1)
                    nc.gpsimd.tensor_tensor(rstd[:, :], mom2[:, :], half[:, :], ALU.pow).then_inc(s_rstd2, 1)
                    pool.wait_ge(s_fin, b + 1)
                    nc.gpsimd.dma_start(out_v[b], pj[:, :, :]).then_inc(s_out, 16)

            for l in range(NLAYER):
                with pool.Fori(0, NB) as b:
                    tail(l, b)

        @block.scalar
        def _(act):
            for l in range(NLAYER):
                act.wait_ge(s_wt, l + 1)
                nc.scalar.activation(wt[:, l, 0:C], misc[0:C, 0:C], ACT.Copy).then_inc(s_wte, 1)
            for l in range(1, NLAYER):
                act.wait_ge(s_wuv, l)
                nc.scalar.activation(wcat[:, l - 1, C:C + 2], misc[0:CE, 0:2], ACT.Copy).then_inc(s_wcat, 1)
            act.wait_ge(s_w0, 1)
            nc.scalar.activation(w0row[:, :, :], misc[:, 0:2 * C].rearrange("p (s c) -> p s c", s=2),
                                 ACT.Copy).then_inc(s_w0e, 1)
            for s in range(2):
                act.wait_ge(s_pt, s + 1)
                nc.scalar.activation(uvrow0[:, s, :], misc[0:NT, 0:P], ACT.Copy).then_inc(s_pte, 1)

            def start_scores(l, b, j, par):
                if not (l == 0 and isinstance(b, int) and b == 0 and j < ES):
                    act.wait_ge(s_p, freed(l, b, j))
                elif j == min(ON_ACT[l]):
                    act.wait_ge(s_prime, 1)
                if j == min(ON_ACT[l]):
                    act.wait_ge(s_ub[par], ub_count(l, b, par))
                nc.scalar.activation(eps[:, j % ES, :], ub[:, par, :], ACT.Relu, bias=v8col[:, j:j + 1],
                                     scale=1.0 - ALPHA).then_inc(s_filla, 1)

            def probs(l, b, j):
                if not (l == 0 and isinstance(b, int) and b == 0 and j < TS):
                    act.wait_ge(s_main, tile(l, b, j) - TS + 1)
                act.wait_ge(s_z, tile(l, b, j) + 1)
                nc.scalar.activation(prob[:, j % TS, :], eps[:, j % ES, :], ACT.Exp,
                                     bias=v2col[:, j:j + 1]).then_inc(s_p, 1)

            def sums_out(l, b, par):
                act.wait_ge(s_main, tile(l, b, NT))
                nc.scalar.activation(acc_s[:, :], acc[0:CE, par, :], ACT.Copy).then_inc(s_acce, 1)

            def tail_exp(l, b):
                act.wait_ge(s_ga, blk(l, b) + 1)
                nc.scalar.activation(e[:, :, :], e[:, :, :], ACT.Exp).then_inc(s_ex, 1)

            def columns_out(l, b):
                act.wait_ge(s_htt, blk(l, b) + 1)
                nc.scalar.activation(ht[0:C, :], misc[0:C, :], ACT.Copy).then_inc(s_hte, 1)

            def products_out(l, b, i):
                act.wait_ge(s_om, 4 * blk(l, b) + i + 1)
                if i < 2:
                    v = misc[:, 0:2 * WC].rearrange("p (r w) -> p r w", w=WC)
                    if l < 2:
                        d = (l + 1) % 2
                        nc.scalar.activation(feat[:, d, bass.ds(b * RT + 2 * i, 2), 0:C], v[:, :, 0:C], ACT.Copy)
                        nc.scalar.activation(vucol[:, d, :, bass.ds(b * RT + 2 * i, 2)].rearrange("p s r -> p r s"),
                                             v[:, :, C:C + 2], ACT.Copy)
                        nc.scalar.activation(vu[:, :, 2 * i:2 * i + 2].rearrange("p s r -> p r s"),
                                             v[:, :, C:C + 2], ACT.Copy)
                    if i == 0:
                        if l == 2 and not (isinstance(b, int) and b == 0):
                            act.wait_ge(s_out, 16 * b)
                        elif not (isinstance(b, int) and b == 0 and l == 0):
                            act.wait_ge(s_y, blk(l, b))
                    nc.scalar.activation(pj[:, 2 * i:2 * i + 2, :], v[:, :, C + 2:WC], ACT.Copy).then_inc(
                        s_oe, 3 if l == 2 and i == 1 else 1)
                elif l < 2:
                    act.wait_ge(s_uvst, 16 + 32 * blk(l, b))
                    nc.scalar.activation(uvrow[:, :], misc[0:2 * RT, 0:P], ACT.Copy).then_inc(s_oe, 2)

            def maxima_out(l, b, par):
                act.wait_ge(s_mt, blk(l, b) + 1)
                nc.scalar.activation(mrow[:, par, :], miscb[0:3, 0:BI], ACT.Copy).then_inc(s_mte, 1)

            def rows_out(l, b, par):
                act.wait_ge(s_cb, blk(l, b) + 1)
                nc.scalar.activation(cb[:, par, :], misc[:, :], ACT.Copy).then_inc(s_cbe, 1)

            def tail_step(l, b, par, t):
                if t == T_EVAC:
                    sums_out(l, b, par)
                if t == T_EXP:
                    tail_exp(l, b)
                if t == T_HTE:
                    columns_out(l, b)
                for i in range(3 if l < 2 else 2):
                    if t == T_OUTE + 2 * i:
                        products_out(l, b, i)

            for l in range(NLAYER):
                act.wait_ge(s_fsum, l + 1)
                nc.scalar.activation(fsum[:, :], misc[:, 0:CE], ACT.Copy).then_inc(s_fsume, 1)
                maxima_out(l, 0, 0)
                rows_out(l, 0, 0)

                def body(b, par, head, tail):
                    for t in range(NT):
                        if t > 0:
                            probs(l, b, t - 1)
                        elif tail:
                            probs(l, b - 1, NT - 1)
                        if t + AHEAD in ON_ACT[l]:
                            start_scores(l, b, t + AHEAD, par)
                        if tail:
                            tail_step(l, b - 1, 1 - par, t)
                        if head and t == T_HEADT:
                            maxima_out(l, b + 1, 1 - par)
                        if head and t == T_ROWS:
                            rows_out(l, b + 1, 1 - par)

                blocks(act, body)
                probs(l, NB - 1, NT - 1)
                for t in range(NT):
                    tail_step(l, NB - 1, 1, t)

        @block.tensor
        def _(pe):
            pe.wait_ge(s_const, 3)
            pe.wait_ge(s_w, 16 * 14)
            pe.wait_ge(s_setup, SEQ_SETUP)
            for l in range(NLAYER):
                if l:
                    pe.wait_ge(s_wte, l)
                nc.tensor.transpose(misc[0:C, 0:C], wld[:, l, :], ident[0:C, 0:C]).then_inc(s_wt, 1)
            for i in range(ES):
                for r in range(RT):
                    mm = nc.tensor.matmul(eps[:, i, r * P:(r + 1) * P], identb[:, :], identb[:, :], start=(r == 0),
                                          stop=(r == RT - 1), skip_group_check=True)
            mm.then_inc(s_prime, 1)
            pe.wait_ge(s_wte, NLAYER)
            for l in range(1, NLAYER):
                if l > 1:
                    pe.wait_ge(s_wcat, l - 1)
                nc.tensor.matmul(misc[0:CE, 0:2], wt[:, l, :], q[:, l, :], start=True, stop=False)
                nc.tensor.matmul(misc[0:CE, 0:2], lbx[:, l - 1, :], attc[:, l - 1, :], start=False,
                                 stop=True).then_inc(s_wuv, 1)
            pe.wait_ge(s_wcat, 2)
            pe.wait_ge(s_q0, 1)
            for s in range(2):
                mm = nc.tensor.matmul(misc[:, s * C:(s + 1) * C], q0[:, s, :], wt[:, 0, 0:C], start=True, stop=True)
            mm.then_inc(s_w0, 1)
            pe.wait_ge(s_w0e, 1)
            for s in range(2):
                if s == 1:
                    pe.wait_ge(s_pte, 1)
                pe.wait_ge(s_prep, 2 * s + 2)
                nc.tensor.transpose(misc[0:NT, 0:P], vucol[:, 0, s, :], ident[:, :]).then_inc(s_pt, 1)

            def wait_started(l, b, j):
                on_act = j in ON_ACT[l]
                pe.wait_ge(s_filla if on_act else s_fill, started(l, b, j, on_act))

            def mask_scores(l, b, j, par):
                on_act = j in ON_ACT[l]
                et = eps[:, j % ES, :]
                c, o = divmod(j * P, CW)
                if on_act:
                    nc.tensor.matmul(et, ones3[:, :], mrow[:, par, :], start=False, stop=False,
                                     skip_group_check=True)
                for r in range(RT):
                    mm = nc.tensor.matmul(et[:, r * P:(r + 1) * P], mask[:, par, c, r, o:o + P].bitcast(FP8),
                                          nbig[:, :], start=False, stop=(r == RT - 1), skip_group_check=True)
                mm.then_inc(s_z, 1)

            def main(l, b, j, par):
                pe.wait_ge(s_p, tile(l, b, j) + 1)
                if j == 0:
                    if not (l == 0 and isinstance(b, int) and b < 2):
                        pe.wait_ge(s_acce, blk(l, b) - 1)
                nc.tensor.matmul(acc[0:CE, par, :], feat[:, l % 2, j, :], prob[:, j % TS, :],
                                 start=(j == 0), stop=(j == NT - 1)).then_inc(s_main, 1)

            def turn_maxima(l, b):
                pe.wait_ge(s_split, blk(l, b) + 1)
                for r in range(RT):
                    mm = nc.tensor.transpose(miscb[0:3, r * P:(r + 1) * P], parts[:, r, 0:3], identb[:, :])
                mm.then_inc(s_mt, 1)

            def spread_maxima(l, b, par):
                pe.wait_ge(s_mte, blk(l, b) + 1)
                nc.tensor.matmul(misc[:, :], ones3[:, :], mrow[:, par, :], start=True, stop=True).then_inc(s_cb, 1)

            def tail_step(l, b, t):
                if t == T_TURN:
                    pe.wait_ge(s_acce, blk(l, b) + 1)
                    for r in range(RT):
                        mm = nc.tensor.transpose(misc[:, r * CE:(r + 1) * CE], acc_s[:, r * P:(r + 1) * P],
                                                 ident[0:CE, 0:CE])
                    mm.then_inc(s_gt, 1)
                if t == T_HT:
                    for r in range(RT):
                        mm = nc.tensor.transpose(misc[0:C, r * P:(r + 1) * P], hn[:, r, :], ident[:, :])
                    mm.then_inc(s_htt, 1)
                for i in range(2):
                    if t == T_OUT + 2 * i:
                        if i == 0:
                            pe.wait_ge(s_hte, blk(l, b) + 1)
                            if not (l == 0 and isinstance(b, int) and b == 0):
                                pe.wait_ge(s_oe, 4 * blk(l, b))
                        else:
                            pe.wait_ge(s_oe, 4 * blk(l, b) + 1)
                        for r in range(2):
                            mm = nc.tensor.matmul(misc[:, r * WC:(r + 1) * WC],
                                                  ht[:, (2 * i + r) * P:(2 * i + r + 1) * P], wcat[:, l, :],
                                                  start=True, stop=True)
                        mm.then_inc(s_om, 3 if l == 2 and i == 1 else 1)
                if t == T_OUT + 4 and l < 2:
                    pe.wait_ge(s_oe, 4 * blk(l, b) + 2)
                    nc.tensor.transpose(misc[0:2 * RT, 0:P], vu[:, :, :].rearrange("p s r -> p (s r)"),
                                        ident[:, :]).then_inc(s_om, 2)

            for l in range(NLAYER):
                if l == 0:
                    pe.wait_ge(s_feat0, 16)
                    pe.wait_ge(s_pte, 2)
                else:
                    pe.wait_ge(s_oe, 4 * blk(l, 0))
                for j in range(NT):
                    mm = nc.tensor.matmul(misc[:, 0:CE], ones[:, :], feat[:, l % 2, j, :], start=(j == 0),
                                          stop=(j == NT - 1))
                mm.then_inc(s_fsum, 1)
                pe.wait_ge(s_fsume, l + 1)
                turn_maxima(l, 0)
                spread_maxima(l, 0, 0)

                def body(b, par, head, tail):
                    for t in range(NT):
                        if tail and t == T_HT:
                            pe.wait_ge(s_h, blk(l, b))
                        wait_started(l, b, t)
                        if t >= LAG:
                            main(l, b, t - LAG, par)
                        elif tail:
                            main(l, b - 1, NT - LAG + t, 1 - par)
                        mask_scores(l, b, t, par)
                        if tail:
                            tail_step(l, b - 1, t)
                        if head and t == T_HEADT:
                            if tail:
                                pe.wait_ge(s_oe, 4 * blk(l, b))
                            turn_maxima(l, b + 1)
                        if head and t == T_ROWS:
                            spread_maxima(l, b + 1, 1 - par)

                blocks(pe, body)
                for t in range(NT - LAG, NT):
                    main(l, NB - 1, t, 1)
                for t in range(NT):
                    if t == T_HT:
                        pe.wait_ge(s_h, blk(l, NB))
                    tail_step(l, NB - 1, t)

        @block.vector
        def _(dve):
            dv = nc.vector

            def step(ins, seq, n):
                ins.then_inc(seq, 1)
                dve.wait_ge(seq, n)

            dve.wait_ge(s_w, 16 * 14)
            for l in range(2):
                for s in range(2):
                    dv.tensor_tensor_reduce(out=acc_s[0:C, (2 * l + s) * HID:(2 * l + s + 1) * HID], in0=lin[:, l, s, :], in1=att[:, l, :], scale=1.0,
                                            scalar=0.0, op0=ALU.mult, op1=ALU.add,
                                            accum_out=q[:, l + 1, 1 - s:2 - s]).then_inc(s_setup, 1)

            dve.wait_ge(s_zero, 12)
            for s in range(2):
                ins = dv.tensor_scalar(q0[:, s, :], ones[0:C, :], q[:, 0, s:s + 1], None, ALU.mult)
            ins.then_inc(s_q0, 1)

            def make_mask(b, par, u):
                c, r = divmod(u, RT)
                dve.wait_ge(s_stage[u % SS], 16 * (b * (UNITS // SS) + u // SS + 1))
                m, o = divmod(u, UNITS // MV)
                if not (isinstance(b, int) and b < 2) and o == 0:
                    dve.wait_ge(s_mst[par * MV + m], 8 * (b - par))
                    dve.wait_ge(s_z, tile(0, b - 1, 0))
                dv.tensor_scalar(mask[:, par, c, r, :], stage[:, u % SS, :], 0, ONE8, ALU.is_le, ALU.mult).then_inc(s_mask, 1)

            def unit_min(l, b, par, u):
                c, r = divmod(u, RT)
                m, o = divmod(u, UNITS // MV)
                if l > 0 and o == 0:
                    landed = 16 * ((b - par) // 2 + 1) if isinstance(b, int) else 8 * (b - par) + 16
                    dve.wait_ge(s_mload[par * MV + m], 16 * (l - 1) * (NB // 2) + landed)
                    dv.memset(st[:, 8 + m:9 + m], 0.0)
                dv.tensor_tensor_reduce(out=junk[:, u % 2, :], in0=mask[:, par, c, r, :], in1=vw[:, c * CW:(c + 1) * CW],
                                        scale=1.0, scalar=2.0, op0=ALU.add, op1=ALU.min,
                                        accum_out=pw[:, r, c:c + 1]).then_inc(s_unit, 1)

            def head(l, b, par, part):
                at = blk(l, b) * SEQ_HEAD
                if part == 0:
                    row_maxima(l, b, par, at)
                if part == 1:
                    split_first(l, b, at)
                if part == 2:
                    split_rest(at)

            def row_maxima(l, b, par, at):
                dve.wait_ge(s_unit, (blk(l, b) + 1) * UNITS)
                step(dv.tensor_reduce(w4[:, :], pw[:, :, :], AX, ALU.min), s_headseq, at + 1)
                step(dv.tensor_scalar(emp[:, par, :], w4[:, :], 1.0, None, ALU.is_ge), s_headseq, at + 2)
                step(dv.scalar_tensor_tensor(ns[:, :], w4[:, :], st[:, 4:5], nuv[:, bass.ds(b * RT, RT)], ALU.mult,
                                             ALU.add), s_headseq, at + 3)
                step(dv.scalar_tensor_tensor(nm[:, :], ns[:, :], ALPHA, ns[:, :], ALU.mult, ALU.min),
                     s_headseq, at + 4)
                step(dv.scalar_tensor_tensor(nm[:, :], vucol[:, l % 2, 1, bass.ds(b * RT, RT)], ALPHA, nm[:, :],
                                             ALU.mult, ALU.add), s_headseq, at + 5)

            def split_first(l, b, at):
                if not (l == 0 and isinstance(b, int) and b == 0):
                    dve.wait_ge(s_mt, blk(l, b))
                step(dv.tensor_copy(parts[:, :, 0], nm[:, :]), s_headseq, at + 6)
                step(dv.tensor_tensor(r1[:, :], nm[:, :], parts[:, :, 0], ALU.subtract), s_headseq, at + 7)

            def split_rest(at):
                step(dv.tensor_copy(parts[:, :, 1], r1[:, :]), s_headseq, at + 8)
                step(dv.tensor_tensor(nm[:, :], r1[:, :], parts[:, :, 1], ALU.subtract), s_headseq, at + 9)
                dv.tensor_copy(parts[:, :, 2], nm[:, :]).then_inc(s_split, 1)

            def spread(a):
                return a.rearrange("p (r o) -> p r o", o=1).broadcast_to([P, RT, C])

            def row_sums_to_means(src, seq, at):
                step(dv.tensor_reduce(mom[:, :], src, AX, ALU.add), seq, at + 1)
                dv.tensor_scalar(mom[:, :], mom[:, :], 1.0 / C, None, ALU.mult).then_inc(seq, 1)

            def variances(src):
                for r in range(RT):
                    ins = dv.tensor_tensor_reduce(out=z[:, r, :], in0=src[:, r, :], in1=src[:, r, :], scale=1.0 / C,
                                                  scalar=EPS, op0=ALU.mult, op1=ALU.add, accum_out=mom2[:, r:r + 1])
                return ins

            def tail_aggregate(l, b, par):
                seq, at = s_tailseq[l], b * SEQ_TAIL[l]
                dve.wait_ge(s_gt, blk(l, b) + 1)
                dve.wait_ge(s_fsume, l + 1)
                for r in range(RT):
                    ins = dv.scalar_tensor_tensor(g[:, r, :], fsum[:, :], emp[:, par, r:r + 1],
                                                  misc[:, r * CE:(r + 1) * CE], ALU.mult, ALU.add)
                step(ins, seq, at + 1)
                dv.reciprocal(rden[:, :], g[:, :, C]).then_inc(seq, 1)

            def tail_elu(l, b):
                seq, at = s_tailseq[l], b * SEQ_TAIL[l]
                dve.wait_ge(seq, at + 2)
                step(dv.tensor_tensor(z[:, :, :], g[:, :, 0:C], spread(rden[:, :]), ALU.mult), seq, at + 3)
                dve.wait_ge(s_xin, 16 * (blk(l, b) + 1))
                if l == 0:
                    step(dv.tensor_tensor(z[:, :, :], z[:, :, :], xin[:, :, 0:C], ALU.add), seq, at + 4)
                if not (l == 0 and isinstance(b, int) and b == 0):
                    dve.wait_ge(s_htt, blk(l, b))
                dv.tensor_scalar(hn[:, :, :], z[:, :, :], 0.0, -1.0, ALU.max, ALU.add)
                dv.tensor_scalar(e[:, :, :], z[:, :, :], 0.0, None, ALU.min).then_inc(s_ga, 1)

            def tail_features(l, b):
                seq, at = s_tailseq[l], b * SEQ_TAIL[l] + (4 if l == 0 else 3)
                dve.wait_ge(s_ex, blk(l, b) + 1)
                step(dv.tensor_tensor(hn[:, :, :], hn[:, :, :], e[:, :, :], ALU.add), seq, at + 1)
                if l == 0:
                    step(dv.tensor_tensor(hn[:, :, :], hn[:, :, :], xin[:, :, 0:C], ALU.add), seq, at + 2)
                    row_sums_to_means(hn[:, :, :], seq, at + 2)
                else:
                    step(dv.tensor_scalar(z[:, :, :], xin[:, :, 0:C], ALPHA, None, ALU.mult), seq, at + 2)
                    dv.scalar_tensor_tensor(hn[:, :, :], hn[:, :, :], 1.0 - ALPHA, z[:, :, :], ALU.mult,
                                            ALU.add).then_inc(s_h, 1)

            def tail_centre(b):
                dve.wait_ge(s_tailseq[0], b * SEQ_TAIL[0] + 8)
                step(dv.tensor_tensor(hn[:, :, :], hn[:, :, :], spread(mom[:, :]), ALU.subtract), s_tailseq[0],
                     b * SEQ_TAIL[0] + 9)
                variances(hn).then_inc(s_mom, 1)

            def tail_norm(b):
                dve.wait_ge(s_rstd, b + 1)
                dv.tensor_tensor(hn[:, :, :], hn[:, :, :], spread(rstd[:, :]), ALU.mult).then_inc(s_h, 1)

            def tail_output(l, b):
                dve.wait_ge(s_oe, 4 * blk(l, b) + 2)
                yb = xin[:, :, C:2 * C]
                if l == 0:
                    dve.wait_ge(s_h, blk(l, b) + 1)
                    dv.tensor_copy(xin[:, :, 0:C], hn[:, :, :])
                    dv.tensor_tensor(yb, hn[:, :, :], pj[:, :, :], ALU.add).then_inc(s_y, 1)
                elif l == 1:
                    dv.tensor_tensor(yb, yb, pj[:, :, :], ALU.add).then_inc(s_y, 1)
                else:
                    seq, at = s_tailseq[l], b * SEQ_TAIL[l] + 5
                    step(dv.tensor_tensor(pj[:, :, :], yb, pj[:, :, :], ALU.add), seq, at + 1)
                    row_sums_to_means(pj[:, :, :], seq, at + 1)
                    dve.wait_ge(seq, at + 3)
                    step(dv.tensor_tensor(pj[:, :, :], pj[:, :, :], spread(mom[:, :]), ALU.subtract), seq, at + 4)
                    variances(pj).then_inc(s_mom2, 1)

            def tail_result(b):
                dve.wait_ge(s_rstd2, b + 1)
                dv.tensor_tensor(pj[:, :, :], pj[:, :, :], spread(rstd[:, :]), ALU.mult).then_inc(s_fin, 1)

            def tail_step(l, b, par, t):
                if t == T_A:
                    tail_aggregate(l, b, par)
                if t == T_A + 1:
                    tail_elu(l, b)
                if t == T_B:
                    tail_features(l, b)
                if t == T_B + 1 and l == 0:
                    tail_centre(b)
                if t == T_C and l == 0:
                    tail_norm(b)
                if t == T_Y:
                    tail_output(l, b)
                if t == T_D and l == 2:
                    tail_result(b)

            def start_scores(l, b, j, par):
                if not (l == 0 and isinstance(b, int) and b == 0 and j < ES):
                    dve.wait_ge(s_p, freed(l, b, j))
                elif j == 0:
                    dve.wait_ge(s_prime, 1)
                dv.scalar_tensor_tensor(eps[:, j % ES, :], ua[:, par, :], v8col[:, j:j + 1], cb[:, par, :],
                                        ALU.add, ALU.max).then_inc(s_fill, 1)

            def add_u(l, b, par):
                dve.wait_ge(s_cbe, blk(l, b) + 1)
                dve.wait_ge(s_ub[par], ub_count(l, b, par))
                dv.scalar_tensor_tensor(ua[:, par, :], ub[:, par, :], 1.0 - ALPHA, cb[:, par, :], ALU.mult,
                                        ALU.add).then_inc(s_ua, 1)

            def node_products(s):
                pr = mask[:, 1, 0:CH // 2, :, :].rearrange("p c r w -> p (c r w)").bitcast(F32).rearrange(
                    "p (t c) -> p t c", c=C)
                w = w0row[:, s, :].rearrange("p (o c) -> p o c", o=1).broadcast_to([P, NT, C])
                step(dv.tensor_tensor(pr, feat[:, s, :, 0:C], w, ALU.mult), s_prep, 2 * s + 1)
                step(dv.tensor_reduce(vucol[:, 0, s, :], pr, AX, ALU.add), s_prep, 2 * s + 2)

            for l in range(NLAYER):
                if l == 0:
                    dve.wait_ge(s_w0e, 1)
                    dve.wait_ge(s_feat0, 16)
                    node_products(0)
                    for u in range(SS):
                        make_mask(0, 0, u)
                    dve.wait_ge(s_x0, 16)
                    node_products(1)
                    for u in range(SS, V_AT):
                        make_mask(0, 0, u)
                at = SEQ_START * l
                dve.wait_ge(s_vb, 16 * (l + 1))
                step(dv.tensor_reduce(st[:, 0:1], vw[:, :], AX, ALU.max), s_startseq, at + 1)
                step(dv.tensor_reduce(st[:, 1:2], vw[:, :], AX, ALU.min), s_startseq, at + 2)
                step(dv.tensor_tensor(st[:, 2:3], st[:, 1:2], st[:, 0:1], ALU.subtract), s_startseq, at + 3)
                step(dv.tensor_scalar(st[:, 2:3], st[:, 2:3], 1.001, -1e-30, ALU.mult, ALU.add), s_startseq, at + 4)
                step(dv.reciprocal(st[:, 3:4], st[:, 2:3]), s_startseq, at + 5)
                step(dv.tensor_scalar(st[:, 4:5], st[:, 2:3], -1.0, None, ALU.mult), s_startseq, at + 6)
                step(dv.tensor_scalar(vw[:, :], vw[:, :], st[:, 0:1], st[:, 3:4], ALU.subtract, ALU.mult),
                     s_startseq, at + 7)
                if l == 0:
                    dve.wait_ge(s_prep, SEQ_PREP)
                else:
                    dve.wait_ge(s_oe, 4 * blk(l, 0))
                step(dv.tensor_scalar(nuv[:, :], vucol[:, l % 2, 1, :], st[:, 0:1], -1.0, ALU.add, ALU.mult),
                     s_startseq, at + 8)
                step(dv.tensor_scalar(v8col[:, :], vucol[:, l % 2, 0, :], 1.0 - ALPHA, None, ALU.mult),
                     s_startseq, at + 9)
                step(dv.tensor_scalar(v2col[:, :], vucol[:, l % 2, 0, :], ALPHA, None, ALU.mult),
                     s_startseq, at + 10)
                for u in range(UNITS):
                    if l == 0 and u + V_AT < UNITS:
                        make_mask(0, 0, u + V_AT)
                    if l == 0:
                        dve.wait_ge(s_mask, u + 1)
                    if l * NB * UNITS + u > 1:
                        dve.wait_ge(s_unit, blk(l, 0) * UNITS + u - 1)
                    unit_min(l, 0, 0, u)
                for part in range(3):
                    head(l, 0, 0, part)
                add_u(l, 0, 0)

                def body(b, par, head_, tail_):
                    for t in range(NT):
                        for u in (UNIT_AT_0 if l == 0 else UNIT_AT).get(t, []) if head_ else []:
                            dve.wait_ge(s_unit, blk(l, b + 1) * UNITS + u - 1)
                        if t == 0:
                            dve.wait_ge(s_ua, blk(l, b) + 1)
                        if t not in ON_ACT[l]:
                            start_scores(l, b, t, par)
                        if tail_:
                            tail_step(l, b - 1, 1 - par, t)
                        if head_:
                            if l == 0:
                                for u in range(UNITS + 1):
                                    if t == u * T_UNITS // UNITS:
                                        if u > 0:
                                            dve.wait_ge(s_mask, (b + 1) * UNITS + u)
                                        if u < UNITS:
                                            make_mask(b + 1, 1 - par, u)
                                        else:
                                            dv.memset(st[:, 8:9], 0.0)
                                        if u > 0:
                                            unit_min(l, b + 1, 1 - par, u - 1)
                            else:
                                for u in UNIT_AT.get(t, []):
                                    unit_min(l, b + 1, 1 - par, u)
                            if T_HEAD <= t < T_HEAD + 3:
                                head(l, b + 1, 1 - par, t - T_HEAD)
                            if t == T_UA:
                                add_u(l, b + 1, 1 - par)

                blocks(dve, body)
                for t in range(NT):
                    tail_step(l, NB - 1, 1, t)


_INS = ["x", "adj", "L0_gnn_entity_embs", "L0_gnn_W", "L0_gnn_a", "L1_gnn_W", "L1_gnn_lin_w", "L1_gnn_lin_b",
        "L1_gnn_attn", "L1_gnn_mlp_w", "L1_gnn_mlp_b"]


def kernel(**inputs):
    import numpy as _np
    import concourse.bacc as _bacc
    from concourse import mybir as _mybir
    from concourse.bass_utils import run_bass_kernel_spmd as _run

    nc = _bacc.Bacc("TRN2", target_bir_lowering=False, num_devices=1)
    arrays, args = {}, []
    for name in _INS:
        a = _np.ascontiguousarray(inputs[name])
        arrays[f"in_{name}_dram"] = a
        args.append(nc.dram_tensor(f"in_{name}_dram", a.shape, _mybir.dt.from_np(a.dtype), kind="ExternalInput").ap())
    args.append(nc.dram_tensor("out_0_dram", (N, C), F32, kind="ExternalOutput").ap())
    build(nc, *args)
    r = _run(nc, [arrays], core_ids=[0])
    return r.results[0]["out_0_dram"]
```

```python
from contextlib import ExitStack

import concourse.bass as bass
from concourse import mybir

ALU = mybir.AluOpType
ACT = mybir.ActivationFunctionType
F32 = mybir.dt.float32
BF16 = mybir.dt.bfloat16
FP8 = mybir.dt.float8e4
I32 = mybir.dt.int32
U8 = mybir.dt.uint8
ONE8 = 56
AX = mybir.AxisListType.X

P = 128
N = 8192
C = 64
HID = 32
CE = C + 1
NT = N // P
BI = 512
RT = BI // P
NB = N // BI
CH = 8
CW = N // CH
UNITS = CH * RT
MV = 4
V_AT = 12
GCH = CH - 1
GT = (GCH * CW // P, NT - GCH * CW // P)
GB = GCH * CW // BI
SS = 8
NLAYER = 3
ALPHA = 0.2
BIG = 9.0e15
EPS = 1e-5
TS = 4
ES = 5
AHEAD = 3
LAG = 3
ACT_TILES = ((1, 2, 4, 5, 6), (2, 4, 6), (2, 4, 6))
ON_ACT = tuple(frozenset(j for j in range(AHEAD, NT) if j % 7 in ks) for ks in ACT_TILES)
WC = 2 * C + 2

SEQ_SETUP = 4
SEQ_PREP = 4
SEQ_STATS = 5
SEQ_START = 2 * SEQ_STATS + 4
SEQ_HEAD = 12
SEQ_TAIL = (9, 5, 9)

T_BOUNDS = 0
T_EARLY = 6
T_EVAC = 6
T_TURN = 8
T_A = 10
T_EXP = 14
T_B = 18
T_C = 20
T_HT = 24
T_HTE = 26
T_OUT = 28
T_OUTE = 30
T_Y = 35
T_D = 39
T_UNITS = 56
T_HEAD = 56
T_HEADT = 58
T_ROWS = 59
T_UA = 63


def unit_slots():
    at = {}
    for u in range(UNITS):
        at.setdefault(u * T_UNITS // UNITS, []).append(u)
    return at


UNIT_AT = unit_slots()
EARLY_AT = {T_EARLY + u * (60 - T_EARLY) // (GCH * RT): [u] for u in range(GCH * RT)}
UNIT_AT_0 = {(u + 1) * T_UNITS // UNITS: [u] for u in range(UNITS)}


def build(nc, x, adj, ent, W0, a0, W12, lin_w, lin_b, attn, mlp_w, mlp_b, out):
    with ExitStack() as ctx:
        def sb(name, shape, dt=F32):
            return ctx.enter_context(nc.sbuf_tensor(name, shape, dt))

        def ps(name, shape, dt=F32):
            return ctx.enter_context(nc.psum_tensor(name, shape, dt))

        def sem(name):
            return ctx.enter_context(nc.semaphore(name))

        mask_d = [nc.dram_tensor(f"mask_d{m}", [NB, P, RT * N // MV], U8).ap() for m in range(MV)]
        uv_d = nc.dram_tensor("uv_d", [NLAYER, 2, N], F32).ap()
        xy_d = nc.dram_tensor("xy_d", [2, N, 2 * C], F32).ap()

        mask = sb("mask", [P, 2, CH, RT, CW], U8)
        stage = sb("stage", [P, SS, CW], I32)
        vw = sb("vw", [P, N])
        feat = sb("feat", [P, 2, NT, CE])
        prob = sb("prob", [P, TS, BI])
        ub = sb("ub", [P, 2, BI])
        cb = sb("cb", [P, 2, BI])
        ua = sb("ua", [P, 2, BI])
        xin = sb("xin", [P, RT, 2 * C])
        acc_s = sb("acc_s", [CE, BI])
        g = sb("g", [P, RT, CE])
        z = sb("z", [P, RT, C])
        e = sb("e", [P, RT, C])
        hn = sb("hn", [P, RT, C])
        ht = sb("ht", [CE, BI])
        uvrow = sb("uvrow", [2 * RT, P])
        uvrow0 = z[0:NT, :, :].rearrange("t r c -> t (r c)").rearrange("t (s p) -> t s p", s=2)
        vu = sb("vu", [P, 2, RT])
        pj = sb("pj", [P, RT, C])
        v8col = sb("v8col", [P, NT])
        v2col = sb("v2col", [P, NT])
        vucol = sb("vucol", [P, 2, 2, NT])
        cm = sb("cm", [P, 2])
        cr = sb("cr", [2, 1])
        dg = sb("dg", [2, 2])
        gst = sb("gst", [P, 4, 2])
        floor = sb("floor", [P, 3])
        st = sb("st", [P, 16])
        fsum = sb("fsum", [P, CE])
        pw = sb("pw", [P, RT, CH])
        w2 = sb("w2", [P, 2, RT])
        vm2 = sb("vm2", [P, 2, RT])
        vm = sb("vm", [P, RT])
        ns = sb("ns", [P, RT])
        nm = sb("nm", [P, RT])
        r1 = sb("r1", [P, RT])
        emp = sb("emp", [P, 2, RT])
        parts = sb("parts", [P, RT, 4], BF16)
        mrow = sb("mrow", [3, 2, BI], BF16)
        rden = sb("rden", [P, RT])
        mom = sb("mom", [P, RT])
        mom2 = sb("mom2", [P, RT])
        half = sb("half", [P, RT])
        rstd = sb("rstd", [P, RT])
        wcat = sb("wcat", [CE, NLAYER, WC])
        w0row = sb("w0row", [P, 2, C])
        q0 = e[0:C, :, :].rearrange("f r c -> f (r c)").rearrange("f (s p) -> f s p", s=2)
        wt = sb("wt", [C, NLAYER, CE])
        q = sb("q", [C, NLAYER, 2])
        lin = sb("lin", [C, 2, 2, HID])
        att = sb("att", [C, 2, HID])
        lbx = sb("lbx", [HID, 2, CE])
        attc = sb("attc", [HID, 2, 2])
        wld = xin[0:C, 0:NLAYER, 0:C]
        junk = sb("junk", [P, 2, CW], U8)
        ident = sb("ident", [P, P])
        identb = sb("identb", [P, P], BF16)
        nbig = sb("nbig", [P, P], BF16)
        ones = sb("ones", [P, P])
        ones3 = sb("ones3", [3, P], BF16)

        eps = ps("eps", [P, ES, BI])
        acc = ps("acc", [P, 2, BI])
        misc = ps("misc", [P, BI])
        miscb = misc[:, :].bitcast(BF16)

        s_w = sem("weights_landed")
        s_zero = sem("memsets_done")
        s_const = sem("constants_done")
        s_wt = sem("w_turned")
        s_wte = sem("w_turned_out")
        s_wuv = sem("wuv_done")
        s_wcat = sem("wcat_done")
        s_x0 = sem("x_landed")
        s_q0 = sem("a_spread")
        s_w0 = sem("w0row_done")
        s_w0e = sem("w0row_out")
        s_prep = sem("prep_steps")
        s_pt = sem("prep_turned")
        s_pte = sem("prep_turned_out")
        s_feat0 = sem("entity_features_landed")
        s_vb = sem("v_rows_landed")
        s_v0 = sem("first_v_stored")
        s_uvst = sem("uv_rows_stored")
        s_fsum = sem("feature_sum_done")
        s_fsume = sem("feature_sum_out")
        s_start = sem("layer_start_done")
        s_stage = [sem(f"adjacency_landed{i}") for i in range(SS)]
        s_mask = sem("mask_unit_made")
        s_unit = sem("unit_minimum_done")
        s_mload = [sem(f"mask_loaded{i}") for i in range(2 * MV)]
        s_mst = [sem(f"mask_stored{i}") for i in range(2 * MV)]
        s_ub = [sem("ub_landed0"), sem("ub_landed1")]
        s_xin = sem("xin_landed")
        s_prime = sem("banks_primed")
        s_fill = sem("scores_started_by_dve")
        s_filla = sem("scores_started_by_act")
        s_z = sem("scores_masked")
        s_p = sem("probs_done")
        s_main = sem("probs_used")
        s_setup = sem("setup_steps")
        s_startseq = sem("layer_start_steps")
        s_colm = sem("v_bounds_by_partition")
        s_cmt = sem("v_bounds_turned")
        s_dg = sem("v_bounds_on_diagonal")
        s_cms = sem("v_bounds_spread")
        s_scale = sem("v_chunk_scaled")
        s_headseq = sem("head_steps")
        s_tailseq = [sem(f"tail_steps{l}") for l in range(NLAYER)]
        s_split = sem("maxima_split")
        s_mt = sem("maxima_turned")
        s_mte = sem("maxima_rows_out")
        s_cb = sem("maxima_spread")
        s_cbe = sem("maxima_spread_out")
        s_ua = sem("ua_done")
        s_acce = sem("sums_out")
        s_gt = sem("sums_turned")
        s_ga = sem("tail_a_done")
        s_ex = sem("tail_exp_done")
        s_mom = sem("variance_done")
        s_rstd = sem("rstd_done")
        s_h = sem("features_done")
        s_htt = sem("features_turned")
        s_hte = sem("features_columns_out")
        s_om = sem("next_products")
        s_oe = sem("next_products_out")
        s_y = sem("output_sums_done")
        s_x1 = sem("x1_stored")
        s_mom2 = sem("last_variance_done")
        s_rstd2 = sem("last_rstd_done")
        s_fin = sem("result_done")
        s_out = sem("result_stored")

        def blk(l, b):
            return l * NB + b

        def tile(l, b, j):
            return (l * NB + b) * NT + j

        def v_count(l, gi):
            return 16 * (2 * l + gi) if l else 16

        def stats_at(l, gi):
            return SEQ_START * l + SEQ_STATS * gi

        def freed(l, b, j):
            if j >= ES:
                return tile(l, b, j) - ES + 1
            last = max(i for i in range(NT) if i % ES == j)
            return tile(l, b, last) - NT + 1

        def started(l, b, j, on_act):
            def some(k, n):
                return sum((i in ON_ACT[k]) == on_act for i in range(n))
            return NB * sum(some(k, NT) for k in range(l)) + b * some(l, NT) + some(l, j + 1)

        def ub_count(l, b, par):
            in_layer = 16 * ((b - par) // 2 + 1) if isinstance(b, int) else 8 * (b - par) + 16
            return 16 * l * (NB // 2) + in_layer

        def blocks(eng, body):
            body(0, 0, True, False)
            body(1, 1, True, True)
            body(2, 0, True, True)
            with eng.Fori(0, (NB - 4) // 2) as k:
                body(2 * k + 3, 1, True, True)
                body(2 * k + 4, 0, True, True)
            body(NB - 1, 1, False, True)

        adj_v = adj.rearrange("(b r p) (c w) -> b c r p w", r=RT, p=P, w=CW)
        x_v = x.rearrange("(b r p) c -> b p r c", r=RT, p=P)
        xy_v = xy_d.rearrange("l (b r p) c -> l b p r c", r=RT, p=P)
        out_v = out.rearrange("(b r p) c -> b p r c", r=RT, p=P)

        block = ctx.enter_context(nc.Block())

        @block.sync
        def _(sp):
            n_w = 0

            def w_load(dst, src):
                sp.dma_start(dst, src).then_inc(s_w, 16)

            sp.wait_ge(s_zero, 4)
            w_load(wld[:, 0, :], W0)
            w_load(wld[:, 1:3, :], W12.rearrange("l f g -> f l g"))
            w_load(wcat[0:C, 0:2, 0:C], W12.rearrange("l f g -> f l g"))
            w_load(wcat[0:C, :, C + 2:WC], mlp_w.rearrange("(l f) g -> f l g", l=NLAYER))
            w_load(wcat[C:CE, 0, C + 2:WC], mlp_b.rearrange("(o g) -> o g", o=1))
            with nc.allow_non_contiguous_dma(reason="a few hundred weights"):
                w_load(q[:, 0, 0:1], a0[C:2 * C, :])
                w_load(q[:, 0, 1:2], a0[0:C, :])
                w_load(lin[:, :, :, :], lin_w.rearrange("l (s f) h -> f l s h", s=2))
                for l in range(2):
                    w_load(att[:, l, :], attn[l].rearrange("h o -> o h").broadcast_to([C, HID]))
                    w_load(lbx[:, l, C:CE], lin_b[l].rearrange("(h o) -> h o", o=1))
                    w_load(attc[:, l, 1:2], attn[l])
            sp.dma_start(feat[:, 0, :, 0:C], ent.rearrange("(t p) c -> p t c", p=P)).then_inc(s_feat0, 16)

            def ub_load(l, b, par):
                if not (l == 0 and isinstance(b, int) and b < 2):
                    sp.wait_ge(s_z, tile(l, b - 1, 0))
                sp.dma_start(ub[:, par, :], uv_d[l, 1:2, bass.ds(b * BI, BI)].broadcast_to([P, BI])).then_inc(
                    s_ub[par], 16)

            def xin_load(l, b):
                if l == 0:
                    sp.dma_start(xin[:, :, 0:C], x_v[b]).then_inc(s_xin, 16)
                else:
                    sp.dma_start(xin[:, :, :], xy_v[l - 1, b]).then_inc(s_xin, 16)

            def xin_free(l, b):
                if isinstance(b, int) and b == 0 and l != 1:
                    return
                if l < 2:
                    sp.wait_ge(s_x1, 16 * blk(l, b))
                else:
                    sp.wait_ge(s_mom2, b)

            def v_load(l, first, last):
                sp.dma_start(vw[:, first:last], uv_d[l, 0:1, first:last].broadcast_to([P, last - first])).then_inc(
                    s_vb, 16)

            def units(l, b, par):
                if not isinstance(b, int):
                    sp.compute_val(b * (P * RT * N // MV))
                for u in range(UNITS):
                    if u == SS and l == 0 and not (isinstance(b, int) and b == 0):
                        ub_load(l, b, par)
                    elif u == SS and l == 0:
                        sp.dma_start(feat[:, 1, :, 0:C], x.rearrange("(t p) c -> p t c", p=P)).then_inc(s_x0, 16)
                    elif u == V_AT and l == 0 and isinstance(b, int) and b == 0:
                        sp.wait_ge(s_v0, 16)
                        v_load(0, 0, N)
                    c, r = divmod(u, RT)
                    if l == 0:
                        if not (isinstance(b, int) and b == 0 and u < SS):
                            sp.wait_ge(s_mask, blk(0, b) * UNITS + u - SS + 1)
                        sp.dma_start(stage[:, u % SS, :], adj_v[b, c, r]).then_inc(s_stage[u % SS], 16)
                        m, o = divmod(u + 1 - RT, UNITS // MV)
                        if m > 0 and o == 0:
                            store(b, m - 1, par)
                    elif u % (UNITS // MV) == 0:
                        m = u // (UNITS // MV)
                        if not (isinstance(b, int) and b < 2):
                            sp.wait_ge(s_z, tile(l, b - 2, (m + 1) * NT // MV))
                        sp.dma_start(moved(par, m), mask_d[m][b]).then_inc(s_mload[par * MV + m], 16)
                if l == 0:
                    store(b, MV - 1, par)

            def moved(par, m):
                w = CH // MV
                return mask[:, par, m * w:(m + 1) * w, :, :].rearrange("p c r w -> p (c r w)")

            def store(b, m, par):
                sp.wait_ge(s_mask, (b * MV + m + 1) * (UNITS // MV))
                sp.dma_start(mask_d[m][b], moved(par, m)).then_inc(s_mst[par * MV + m], 16)

            for l in range(NLAYER):
                if l == 0:
                    units(0, 0, 0)
                    sp.wait_ge(s_uvst, 16)
                else:
                    sp.wait_ge(s_z, tile(l, 0, 0))
                    if l == 1:
                        for i in range(2 * MV):
                            sp.wait_ge(s_mst[i], 16 * NB // 2)
                    sp.wait_ge(s_uvst, 16 + 32 * NB * l)
                    v_load(l, GCH * CW, N)
                    sp.wait_ge(s_x1, 16 * NB * l)
                ub_load(l, 0, 0)

                def body(b, par, head, tail):
                    if tail:
                        xin_free(l, b - 1)
                        xin_load(l, b - 1)
                    if head:
                        units(l, b + 1, 1 - par)
                        if l > 0:
                            ub_load(l, b + 1, 1 - par)
                    elif l < NLAYER - 1:
                        sp.wait_ge(s_uvst, 16 + 32 * (blk(l, 0) + GB))
                        sp.wait_ge(s_unit, blk(l + 1, 0) * UNITS)
                        v_load(l + 1, 0, GCH * CW)
                        sp.wait_ge(s_z, tile(l, b, 0))
                        if l == 0:
                            for m in range(MV):
                                sp.wait_ge(s_mst[m], 16 * NB // 2)
                        units(l + 1, 0, 0)

                blocks(sp, body)
                xin_free(l, NB - 1)
                xin_load(l, NB - 1)
            for i in range(2 * MV):
                sp.wait_ge(s_mst[i], 16 * NB // 2)
            sp.wait_ge(s_uvst, 16 + 32 * 2 * NB)
            sp.wait_ge(s_x1, 16 * 2 * NB)
            sp.wait_ge(s_out, 16 * NB)

        @block.gpsimd
        def _(pool):
            for n, (m, v) in enumerate((
                    (wcat[:, :, :], 0.0), (wt[:, :, :], 0.0), (lbx[:, :, :], 0.0), (attc[:, :, :], 0.0),
                    (half[:, :], -0.5), (ones[:, :], 1.0), (ones3[:, :], 1.0), (ht[C:CE, :], 1.0),
                    (feat[:, :, :, C:CE], 1.0), (identb[:, :], 0.0), (nbig[:, :], 0.0), (ident[:, :], 0.0))):
                nc.gpsimd.memset(m, v).then_inc(s_zero, 1)
                pool.wait_ge(s_zero, n + 1)
            for m, v in ((ident, 1.0), (identb, 1.0), (nbig, -BIG)):
                nc.gpsimd.affine_select(out=m[:, :], in_=m[:, :], compare_op=ALU.not_equal, fill=v, base=0,
                                        pattern=[[-1, P]], channel_multiplier=1).then_inc(s_const, 1)
            for s in range(2):
                pool.wait_ge(s_pte, s + 1)
                nc.gpsimd.dma_start(uv_d[0, s].rearrange("(t p) -> t p", p=P), uvrow0[:, s, :]).then_inc(
                    s_uvst if s else s_v0, 16)

            def tail(l, b):
                if l == 0:
                    pool.wait_ge(s_mom, blk(l, b) + 1)
                    nc.gpsimd.tensor_tensor(rstd[:, :], mom2[:, :], half[:, :], ALU.pow).then_inc(s_rstd, 1)
                if l < 2:
                    pool.wait_ge(s_oe, 4 * blk(l, b) + 4)
                    for s in range(2):
                        nc.gpsimd.dma_start(
                            uv_d[l + 1, s, bass.ds(b * BI, BI)].rearrange("(r p) -> r p", p=P),
                            uvrow[s * RT:(s + 1) * RT, :]).then_inc(s_uvst, 16)
                    pool.wait_ge(s_y, blk(l, b) + 1)
                    nc.gpsimd.dma_start(xy_v[l, b], xin[:, :, :]).then_inc(s_x1, 16)
                else:
                    pool.wait_ge(s_mom2, b + 1)
                    nc.gpsimd.tensor_tensor(rstd[:, :], mom2[:, :], half[:, :], ALU.pow).then_inc(s_rstd2, 1)
                    pool.wait_ge(s_fin, b + 1)
                    nc.gpsimd.dma_start(out_v[b], pj[:, :, :]).then_inc(s_out, 16)

            for l in range(NLAYER):
                with pool.Fori(0, NB) as b:
                    tail(l, b)

        @block.scalar
        def _(act):
            for l in range(NLAYER):
                act.wait_ge(s_wt, l + 1)
                nc.scalar.activation(wt[:, l, 0:C], misc[0:C, 0:C], ACT.Copy).then_inc(s_wte, 1)
            for l in range(1, NLAYER):
                act.wait_ge(s_wuv, l)
                nc.scalar.activation(wcat[:, l - 1, C:C + 2], misc[0:CE, 0:2], ACT.Copy).then_inc(s_wcat, 1)
            act.wait_ge(s_w0, 1)
            nc.scalar.activation(w0row[:, :, :], misc[:, 0:2 * C].rearrange("p (s c) -> p s c", s=2),
                                 ACT.Copy).then_inc(s_w0e, 1)
            for s in range(2):
                act.wait_ge(s_pt, s + 1)
                nc.scalar.activation(uvrow0[:, s, :], misc[0:NT, 0:P], ACT.Copy).then_inc(s_pte, 1)

            def start_scores(l, b, j, par):
                if not (l == 0 and isinstance(b, int) and b == 0 and j < ES):
                    act.wait_ge(s_p, freed(l, b, j))
                elif j == min(ON_ACT[l]):
                    act.wait_ge(s_prime, 1)
                if j == min(ON_ACT[l]):
                    act.wait_ge(s_ub[par], ub_count(l, b, par))
                nc.scalar.activation(eps[:, j % ES, :], ub[:, par, :], ACT.Relu, bias=v8col[:, j:j + 1],
                                     scale=1.0 - ALPHA).then_inc(s_filla, 1)

            def probs(l, b, j):
                if not (l == 0 and isinstance(b, int) and b == 0 and j < TS):
                    act.wait_ge(s_main, tile(l, b, j) - TS + 1)
                act.wait_ge(s_z, tile(l, b, j) + 1)
                nc.scalar.activation(prob[:, j % TS, :], eps[:, j % ES, :], ACT.Exp,
                                     bias=v2col[:, j:j + 1]).then_inc(s_p, 1)

            def sums_out(l, b, par):
                act.wait_ge(s_main, tile(l, b, NT))
                nc.scalar.activation(acc_s[:, :], acc[0:CE, par, :], ACT.Copy).then_inc(s_acce, 1)

            def tail_exp(l, b):
                act.wait_ge(s_ga, blk(l, b) + 1)
                nc.scalar.activation(e[:, :, :], e[:, :, :], ACT.Exp).then_inc(s_ex, 1)

            def columns_out(l, b):
                act.wait_ge(s_htt, blk(l, b) + 1)
                nc.scalar.activation(ht[0:C, :], misc[0:C, :], ACT.Copy).then_inc(s_hte, 1)

            def products_out(l, b, i):
                act.wait_ge(s_om, 4 * blk(l, b) + i + 1)
                if i < 2:
                    v = misc[:, 0:2 * WC].rearrange("p (r w) -> p r w", w=WC)
                    if l < 2:
                        d = (l + 1) % 2
                        nc.scalar.activation(feat[:, d, bass.ds(b * RT + 2 * i, 2), 0:C], v[:, :, 0:C], ACT.Copy)
                        nc.scalar.activation(vucol[:, d, :, bass.ds(b * RT + 2 * i, 2)].rearrange("p s r -> p r s"),
                                             v[:, :, C:C + 2], ACT.Copy)
                        nc.scalar.activation(vu[:, :, 2 * i:2 * i + 2].rearrange("p s r -> p r s"),
                                             v[:, :, C:C + 2], ACT.Copy)
                    if i == 0:
                        if l == 2 and not (isinstance(b, int) and b == 0):
                            act.wait_ge(s_out, 16 * b)
                        elif not (isinstance(b, int) and b == 0 and l == 0):
                            act.wait_ge(s_y, blk(l, b))
                    nc.scalar.activation(pj[:, 2 * i:2 * i + 2, :], v[:, :, C + 2:WC], ACT.Copy).then_inc(
                        s_oe, 3 if l == 2 and i == 1 else 1)
                elif l < 2:
                    act.wait_ge(s_uvst, 16 + 32 * blk(l, b))
                    nc.scalar.activation(uvrow[:, :], misc[0:2 * RT, 0:P], ACT.Copy).then_inc(s_oe, 2)

            def maxima_out(l, b, par):
                act.wait_ge(s_mt, blk(l, b) + 1)
                nc.scalar.activation(mrow[:, par, :], miscb[0:3, 0:BI], ACT.Copy).then_inc(s_mte, 1)

            def rows_out(l, b, par):
                act.wait_ge(s_cb, blk(l, b) + 1)
                nc.scalar.activation(cb[:, par, :], misc[:, :], ACT.Copy).then_inc(s_cbe, 1)

            def tail_step(l, b, par, t):
                if t == T_EVAC:
                    sums_out(l, b, par)
                if t == T_EXP:
                    tail_exp(l, b)
                if t == T_HTE:
                    columns_out(l, b)
                for i in range(3 if l < 2 else 2):
                    if t == T_OUTE + 2 * i:
                        products_out(l, b, i)

            for l in range(NLAYER):
                act.wait_ge(s_fsum, l + 1)
                nc.scalar.activation(fsum[:, :], misc[:, 0:CE], ACT.Copy).then_inc(s_fsume, 1)
                maxima_out(l, 0, 0)
                rows_out(l, 0, 0)

                def body(b, par, head, tail):
                    for t in range(NT):
                        if t > 0:
                            probs(l, b, t - 1)
                        elif tail:
                            probs(l, b - 1, NT - 1)
                        if t + AHEAD in ON_ACT[l]:
                            start_scores(l, b, t + AHEAD, par)
                        if tail:
                            tail_step(l, b - 1, 1 - par, t)
                        if head and t == T_HEADT:
                            maxima_out(l, b + 1, 1 - par)
                        if head and t == T_ROWS:
                            rows_out(l, b + 1, 1 - par)

                blocks(act, body)
                probs(l, NB - 1, NT - 1)
                for t in range(NT):
                    tail_step(l, NB - 1, 1, t)

        @block.tensor
        def _(pe):
            pe.wait_ge(s_const, 3)
            pe.wait_ge(s_w, 16 * 14)
            pe.wait_ge(s_setup, SEQ_SETUP)
            for l in range(NLAYER):
                if l:
                    pe.wait_ge(s_wte, l)
                nc.tensor.transpose(misc[0:C, 0:C], wld[:, l, :], ident[0:C, 0:C]).then_inc(s_wt, 1)
            for i in range(ES):
                for r in range(RT):
                    mm = nc.tensor.matmul(eps[:, i, r * P:(r + 1) * P], identb[:, :], identb[:, :], start=(r == 0),
                                          stop=(r == RT - 1), skip_group_check=True)
            mm.then_inc(s_prime, 1)
            pe.wait_ge(s_wte, NLAYER)
            for l in range(1, NLAYER):
                if l > 1:
                    pe.wait_ge(s_wcat, l - 1)
                nc.tensor.matmul(misc[0:CE, 0:2], wt[:, l, :], q[:, l, :], start=True, stop=False)
                nc.tensor.matmul(misc[0:CE, 0:2], lbx[:, l - 1, :], attc[:, l - 1, :], start=False,
                                 stop=True).then_inc(s_wuv, 1)
            pe.wait_ge(s_wcat, 2)
            pe.wait_ge(s_q0, 1)
            for s in range(2):
                mm = nc.tensor.matmul(misc[:, s * C:(s + 1) * C], q0[:, s, :], wt[:, 0, 0:C], start=True, stop=True)
            mm.then_inc(s_w0, 1)
            pe.wait_ge(s_w0e, 1)

            def wait_started(l, b, j):
                on_act = j in ON_ACT[l]
                pe.wait_ge(s_filla if on_act else s_fill, started(l, b, j, on_act))

            def mask_scores(l, b, j, par):
                on_act = j in ON_ACT[l]
                et = eps[:, j % ES, :]
                c, o = divmod(j * P, CW)
                if on_act:
                    nc.tensor.matmul(et, ones3[:, :], mrow[:, par, :], start=False, stop=False,
                                     skip_group_check=True)
                for r in range(RT):
                    mm = nc.tensor.matmul(et[:, r * P:(r + 1) * P], mask[:, par, c, r, o:o + P].bitcast(FP8),
                                          nbig[:, :], start=False, stop=(r == RT - 1), skip_group_check=True)
                mm.then_inc(s_z, 1)

            def main(l, b, j, par):
                pe.wait_ge(s_p, tile(l, b, j) + 1)
                if j == 0:
                    if not (l == 0 and isinstance(b, int) and b < 2):
                        pe.wait_ge(s_acce, blk(l, b) - 1)
                nc.tensor.matmul(acc[0:CE, par, :], feat[:, l % 2, j, :], prob[:, j % TS, :],
                                 start=(j == 0), stop=(j == NT - 1)).then_inc(s_main, 1)

            def turn_bounds(l, gi):
                pe.wait_ge(s_colm, 2 * l + gi + 1)
                nc.tensor.transpose(misc[0:2, 0:P], cm[:, :], ident[:, :]).then_inc(s_cmt, 1)

            def spread_bounds(l, gi):
                pe.wait_ge(s_dg, 2 * l + gi + 1)
                nc.tensor.matmul(misc[:, 0:2], ones[0:2, :], dg[:, :], start=True, stop=True).then_inc(s_cms, 1)

            def bounds_read(l, gi):
                pe.wait_ge(s_startseq, stats_at(l, gi) + 2)

            for s in range(2):
                pe.wait_ge(s_prep, 2 * s + 2)
                nc.tensor.transpose(misc[0:NT, 0:P], vucol[:, 0, s, :], ident[:, :]).then_inc(s_pt, 1)
                pe.wait_ge(s_pte, s + 1)
                if s == 0:
                    for gi in range(2):
                        turn_bounds(0, gi)
                        spread_bounds(0, gi)
                        bounds_read(0, gi)

            def turn_maxima(l, b):
                pe.wait_ge(s_split, blk(l, b) + 1)
                for r in range(RT):
                    mm = nc.tensor.transpose(miscb[0:3, r * P:(r + 1) * P], parts[:, r, 0:3], identb[:, :])
                mm.then_inc(s_mt, 1)

            def spread_maxima(l, b, par):
                pe.wait_ge(s_mte, blk(l, b) + 1)
                nc.tensor.matmul(misc[:, :], ones3[:, :], mrow[:, par, :], start=True, stop=True).then_inc(s_cb, 1)

            def tail_step(l, b, t):
                if t == T_TURN:
                    pe.wait_ge(s_acce, blk(l, b) + 1)
                    for r in range(RT):
                        mm = nc.tensor.transpose(misc[:, r * CE:(r + 1) * CE], acc_s[:, r * P:(r + 1) * P],
                                                 ident[0:CE, 0:CE])
                    mm.then_inc(s_gt, 1)
                if t == T_HT:
                    for r in range(RT):
                        mm = nc.tensor.transpose(misc[0:C, r * P:(r + 1) * P], hn[:, r, :], ident[:, :])
                    mm.then_inc(s_htt, 1)
                for i in range(2):
                    if t == T_OUT + 2 * i:
                        if i == 0:
                            pe.wait_ge(s_hte, blk(l, b) + 1)
                            if not (l == 0 and isinstance(b, int) and b == 0):
                                pe.wait_ge(s_oe, 4 * blk(l, b))
                        else:
                            pe.wait_ge(s_oe, 4 * blk(l, b) + 1)
                        for r in range(2):
                            mm = nc.tensor.matmul(misc[:, r * WC:(r + 1) * WC],
                                                  ht[:, (2 * i + r) * P:(2 * i + r + 1) * P], wcat[:, l, :],
                                                  start=True, stop=True)
                        mm.then_inc(s_om, 3 if l == 2 and i == 1 else 1)
                if t == T_OUT + 4 and l < 2:
                    pe.wait_ge(s_oe, 4 * blk(l, b) + 2)
                    nc.tensor.transpose(misc[0:2 * RT, 0:P], vu[:, :, :].rearrange("p s r -> p (s r)"),
                                        ident[:, :]).then_inc(s_om, 2)

            for l in range(NLAYER):
                if l == 0:
                    pe.wait_ge(s_feat0, 16)
                else:
                    pe.wait_ge(s_oe, 4 * blk(l, 0))
                    turn_bounds(l, 1)
                    spread_bounds(l, 1)
                    bounds_read(l, 1)
                for j in range(NT):
                    mm = nc.tensor.matmul(misc[:, 0:CE], ones[:, :], feat[:, l % 2, j, :], start=(j == 0),
                                          stop=(j == NT - 1))
                mm.then_inc(s_fsum, 1)
                pe.wait_ge(s_fsume, l + 1)
                turn_maxima(l, 0)
                spread_maxima(l, 0, 0)

                def body(b, par, head, tail):
                    for t in range(NT):
                        if tail and t == T_HT:
                            pe.wait_ge(s_h, blk(l, b))
                        wait_started(l, b, t)
                        if t >= LAG:
                            main(l, b, t - LAG, par)
                        elif tail:
                            main(l, b - 1, NT - LAG + t, 1 - par)
                        mask_scores(l, b, t, par)
                        if not head and l < NLAYER - 1:
                            if t == T_BOUNDS + 1:
                                pe.wait_ge(s_cbe, blk(l, b) + 1)
                                turn_bounds(l + 1, 0)
                            if t == T_BOUNDS + 3:
                                spread_bounds(l + 1, 0)
                            if t == T_TURN:
                                bounds_read(l + 1, 0)
                        if tail:
                            tail_step(l, b - 1, t)
                        if head and t == T_HEADT:
                            if tail:
                                pe.wait_ge(s_oe, 4 * blk(l, b))
                            turn_maxima(l, b + 1)
                        if head and t == T_ROWS:
                            spread_maxima(l, b + 1, 1 - par)

                blocks(pe, body)
                for t in range(NT - LAG, NT):
                    main(l, NB - 1, t, 1)
                for t in range(NT):
                    if t == T_HT:
                        pe.wait_ge(s_h, blk(l, NB))
                    tail_step(l, NB - 1, t)

        @block.vector
        def _(dve):
            dv = nc.vector

            def step(ins, seq, n):
                ins.then_inc(seq, 1)
                dve.wait_ge(seq, n)

            dve.wait_ge(s_w, 16 * 14)
            for l in range(2):
                for s in range(2):
                    dv.tensor_tensor_reduce(out=acc_s[0:C, (2 * l + s) * HID:(2 * l + s + 1) * HID], in0=lin[:, l, s, :], in1=att[:, l, :], scale=1.0,
                                            scalar=0.0, op0=ALU.mult, op1=ALU.add,
                                            accum_out=q[:, l + 1, 1 - s:2 - s]).then_inc(s_setup, 1)

            dve.wait_ge(s_zero, 12)
            for s in range(2):
                ins = dv.tensor_scalar(q0[:, s, :], ones[0:C, :], q[:, 0, s:s + 1], None, ALU.mult)
            ins.then_inc(s_q0, 1)

            def make_mask(b, par, u):
                c, r = divmod(u, RT)
                dve.wait_ge(s_stage[u % SS], 16 * (b * (UNITS // SS) + u // SS + 1))
                m, o = divmod(u, UNITS // MV)
                if not (isinstance(b, int) and b < 2) and o == 0:
                    dve.wait_ge(s_mst[par * MV + m], 8 * (b - par))
                    dve.wait_ge(s_z, tile(0, b - 2, (m + 1) * NT // MV))
                dv.tensor_scalar(mask[:, par, c, r, :], stage[:, u % SS, :], 0, ONE8, ALU.is_le, ALU.mult).then_inc(s_mask, 1)

            def unit_min(l, b, par, u):
                c, r = divmod(u, RT)
                m, o = divmod(u, UNITS // MV)
                if l > 0 and o == 0:
                    landed = 16 * ((b - par) // 2 + 1) if isinstance(b, int) else 8 * (b - par) + 16
                    dve.wait_ge(s_mload[par * MV + m], 16 * (l - 1) * (NB // 2) + landed)
                    dv.memset(st[:, 8 + m:9 + m], 0.0)
                dv.tensor_tensor_reduce(out=junk[:, u % 2, :], in0=mask[:, par, c, r, :], in1=vw[:, c * CW:(c + 1) * CW],
                                        scale=1.0, scalar=2.0, op0=ALU.add, op1=ALU.min,
                                        accum_out=pw[:, r, c:c + 1]).then_inc(s_unit, 1)

            def head(l, b, par, part):
                at = blk(l, b) * SEQ_HEAD
                if part == 0:
                    row_maxima(l, b, par, at)
                if part == 1:
                    split_first(l, b, at)
                if part == 2:
                    split_rest(at)

            def row_maxima(l, b, par, at):
                dve.wait_ge(s_unit, (blk(l, b) + 1) * UNITS)
                u = vucol[:, l % 2, 1, bass.ds(b * RT, RT)]
                dv.tensor_copy(w2[:, 1, :], pw[:, :, GCH])
                step(dv.tensor_reduce(w2[:, 0, :], pw[:, :, 0:GCH], AX, ALU.min), s_headseq, at + 1)
                for gi in range(2):
                    ins = dv.tensor_scalar(vm2[:, gi, :], w2[:, gi, :], gst[:, 2, gi:gi + 1], gst[:, 0, gi:gi + 1],
                                           ALU.mult, ALU.add)
                step(ins, s_headseq, at + 2)
                step(dv.tensor_scalar(w2[:, :, :], w2[:, :, :], 1.0, -3e38, ALU.is_ge, ALU.mult), s_headseq, at + 3)
                step(dv.tensor_tensor(vm2[:, :, :], vm2[:, :, :], w2[:, :, :], ALU.add), s_headseq, at + 4)
                step(dv.tensor_tensor(vm[:, :], vm2[:, 0, :], vm2[:, 1, :], ALU.max), s_headseq, at + 5)
                dv.tensor_scalar(emp[:, par, :], vm[:, :], -1e38, None, ALU.is_le)
                step(dv.scalar_tensor_tensor(ns[:, :], vm[:, :], floor[:, 2:3], u, ALU.max, ALU.add),
                     s_headseq, at + 6)
                step(dv.scalar_tensor_tensor(nm[:, :], ns[:, :], ALPHA, ns[:, :], ALU.mult, ALU.max),
                     s_headseq, at + 7)
                step(dv.scalar_tensor_tensor(nm[:, :], u, ALPHA, nm[:, :], ALU.mult, ALU.subtract),
                     s_headseq, at + 8)

            def split_first(l, b, at):
                if not (l == 0 and isinstance(b, int) and b == 0):
                    dve.wait_ge(s_mt, blk(l, b))
                step(dv.tensor_copy(parts[:, :, 0], nm[:, :]), s_headseq, at + 9)
                step(dv.tensor_tensor(r1[:, :], nm[:, :], parts[:, :, 0], ALU.subtract), s_headseq, at + 10)

            def split_rest(at):
                step(dv.tensor_copy(parts[:, :, 1], r1[:, :]), s_headseq, at + 11)
                step(dv.tensor_tensor(nm[:, :], r1[:, :], parts[:, :, 1], ALU.subtract), s_headseq, at + 12)
                dv.tensor_copy(parts[:, :, 2], nm[:, :]).then_inc(s_split, 1)

            def spread(a):
                return a.rearrange("p (r o) -> p r o", o=1).broadcast_to([P, RT, C])

            def row_sums_to_means(src, seq, at):
                step(dv.tensor_reduce(mom[:, :], src, AX, ALU.add), seq, at + 1)
                dv.tensor_scalar(mom[:, :], mom[:, :], 1.0 / C, None, ALU.mult).then_inc(seq, 1)

            def variances(src):
                for r in range(RT):
                    ins = dv.tensor_tensor_reduce(out=z[:, r, :], in0=src[:, r, :], in1=src[:, r, :], scale=1.0 / C,
                                                  scalar=EPS, op0=ALU.mult, op1=ALU.add, accum_out=mom2[:, r:r + 1])
                return ins

            def tail_aggregate(l, b, par):
                seq, at = s_tailseq[l], b * SEQ_TAIL[l]
                dve.wait_ge(s_gt, blk(l, b) + 1)
                dve.wait_ge(s_fsume, l + 1)
                for r in range(RT):
                    ins = dv.scalar_tensor_tensor(g[:, r, :], fsum[:, :], emp[:, par, r:r + 1],
                                                  misc[:, r * CE:(r + 1) * CE], ALU.mult, ALU.add)
                step(ins, seq, at + 1)
                dv.reciprocal(rden[:, :], g[:, :, C]).then_inc(seq, 1)

            def tail_elu(l, b):
                seq, at = s_tailseq[l], b * SEQ_TAIL[l]
                dve.wait_ge(seq, at + 2)
                step(dv.tensor_tensor(z[:, :, :], g[:, :, 0:C], spread(rden[:, :]), ALU.mult), seq, at + 3)
                dve.wait_ge(s_xin, 16 * (blk(l, b) + 1))
                if l == 0:
                    step(dv.tensor_tensor(z[:, :, :], z[:, :, :], xin[:, :, 0:C], ALU.add), seq, at + 4)
                if not (l == 0 and isinstance(b, int) and b == 0):
                    dve.wait_ge(s_htt, blk(l, b))
                dv.tensor_scalar(hn[:, :, :], z[:, :, :], 0.0, -1.0, ALU.max, ALU.add)
                dv.tensor_scalar(e[:, :, :], z[:, :, :], 0.0, None, ALU.min).then_inc(s_ga, 1)

            def tail_features(l, b):
                seq, at = s_tailseq[l], b * SEQ_TAIL[l] + (4 if l == 0 else 3)
                dve.wait_ge(s_ex, blk(l, b) + 1)
                step(dv.tensor_tensor(hn[:, :, :], hn[:, :, :], e[:, :, :], ALU.add), seq, at + 1)
                if l == 0:
                    step(dv.tensor_tensor(hn[:, :, :], hn[:, :, :], xin[:, :, 0:C], ALU.add), seq, at + 2)
                    row_sums_to_means(hn[:, :, :], seq, at + 2)
                else:
                    step(dv.tensor_scalar(z[:, :, :], xin[:, :, 0:C], ALPHA, None, ALU.mult), seq, at + 2)
                    dv.scalar_tensor_tensor(hn[:, :, :], hn[:, :, :], 1.0 - ALPHA, z[:, :, :], ALU.mult,
                                            ALU.add).then_inc(s_h, 1)

            def tail_centre(b):
                dve.wait_ge(s_tailseq[0], b * SEQ_TAIL[0] + 8)
                step(dv.tensor_tensor(hn[:, :, :], hn[:, :, :], spread(mom[:, :]), ALU.subtract), s_tailseq[0],
                     b * SEQ_TAIL[0] + 9)
                variances(hn).then_inc(s_mom, 1)

            def tail_norm(b):
                dve.wait_ge(s_rstd, b + 1)
                dv.tensor_tensor(hn[:, :, :], hn[:, :, :], spread(rstd[:, :]), ALU.mult).then_inc(s_h, 1)

            def tail_output(l, b):
                dve.wait_ge(s_oe, 4 * blk(l, b) + 2)
                yb = xin[:, :, C:2 * C]
                if l == 0:
                    dve.wait_ge(s_h, blk(l, b) + 1)
                    dv.tensor_copy(xin[:, :, 0:C], hn[:, :, :])
                    dv.tensor_tensor(yb, hn[:, :, :], pj[:, :, :], ALU.add).then_inc(s_y, 1)
                elif l == 1:
                    dv.tensor_tensor(yb, yb, pj[:, :, :], ALU.add).then_inc(s_y, 1)
                else:
                    seq, at = s_tailseq[l], b * SEQ_TAIL[l] + 5
                    step(dv.tensor_tensor(pj[:, :, :], yb, pj[:, :, :], ALU.add), seq, at + 1)
                    row_sums_to_means(pj[:, :, :], seq, at + 1)
                    dve.wait_ge(seq, at + 3)
                    step(dv.tensor_tensor(pj[:, :, :], pj[:, :, :], spread(mom[:, :]), ALU.subtract), seq, at + 4)
                    variances(pj).then_inc(s_mom2, 1)

            def tail_result(b):
                dve.wait_ge(s_rstd2, b + 1)
                dv.tensor_tensor(pj[:, :, :], pj[:, :, :], spread(rstd[:, :]), ALU.mult).then_inc(s_fin, 1)

            def tail_step(l, b, par, t):
                if t == T_A:
                    tail_aggregate(l, b, par)
                if t == T_A + 1:
                    tail_elu(l, b)
                if t == T_B:
                    tail_features(l, b)
                if t == T_B + 1 and l == 0:
                    tail_centre(b)
                if t == T_C and l == 0:
                    tail_norm(b)
                if t == T_Y:
                    tail_output(l, b)
                if t == T_D and l == 2:
                    tail_result(b)

            def start_scores(l, b, j, par):
                if not (l == 0 and isinstance(b, int) and b == 0 and j < ES):
                    dve.wait_ge(s_p, freed(l, b, j))
                elif j == 0:
                    dve.wait_ge(s_prime, 1)
                dv.scalar_tensor_tensor(eps[:, j % ES, :], ua[:, par, :], v8col[:, j:j + 1], cb[:, par, :],
                                        ALU.add, ALU.max).then_inc(s_fill, 1)

            def add_u(l, b, par):
                dve.wait_ge(s_cbe, blk(l, b) + 1)
                dve.wait_ge(s_ub[par], ub_count(l, b, par))
                dv.scalar_tensor_tensor(ua[:, par, :], ub[:, par, :], 1.0 - ALPHA, cb[:, par, :], ALU.mult,
                                        ALU.add).then_inc(s_ua, 1)

            def node_products(s):
                pr = mask[:, 1, 0:CH // 2, :, :].rearrange("p c r w -> p (c r w)").bitcast(F32).rearrange(
                    "p (t c) -> p t c", c=C)
                w = w0row[:, s, :].rearrange("p (o c) -> p o c", o=1).broadcast_to([P, NT, C])
                step(dv.tensor_tensor(pr, feat[:, s, :, 0:C], w, ALU.mult), s_prep, 2 * s + 1)
                step(dv.tensor_reduce(vucol[:, 0, s, :], pr, AX, ALU.add), s_prep, 2 * s + 2)

            def bounds(l, gi, part):
                at = stats_at(l, gi)
                if part == 0:
                    v = vucol[:, l % 2, 0, GT[0] * gi:GT[0] + GT[1] * gi]
                    dv.tensor_reduce(cm[:, 0:1], v, AX, ALU.max)
                    dv.tensor_reduce(cm[:, 1:2], v, AX, ALU.min, negate=True).then_inc(s_colm, 1)
                if part == 1:
                    dve.wait_ge(s_cmt, 2 * l + gi + 1)
                    step(dv.tensor_reduce(cr[:, :], misc[0:2, 0:P], AX, ALU.max), s_startseq, at + 1)
                    dv.tensor_scalar(dg[:, :], ident[0:2, 0:2], cr[:, :], None, ALU.mult).then_inc(s_dg, 1)
                if part == 2:
                    dve.wait_ge(s_cms, 2 * l + gi + 1)
                    step(dv.tensor_copy(gst[:, 0:2, gi], misc[:, 0:2]), s_startseq, at + 2)
                    step(dv.tensor_tensor(gst[:, 2, gi:gi + 1], gst[:, 0, gi:gi + 1], gst[:, 1, gi:gi + 1], ALU.add),
                         s_startseq, at + 3)
                    step(dv.tensor_scalar(gst[:, 2, gi:gi + 1], gst[:, 2, gi:gi + 1], -1.001, -1e-30, ALU.mult,
                                          ALU.add), s_startseq, at + 4)
                    step(dv.reciprocal(gst[:, 3, gi:gi + 1], gst[:, 2, gi:gi + 1]), s_startseq, at + 5)

            def scale(l, c):
                gi = 0 if c < GCH else 1
                w = vw[:, c * CW:(c + 1) * CW]
                dve.wait_ge(s_vb, v_count(l, gi))
                step(dv.tensor_scalar(w, w, gst[:, 0, gi:gi + 1], gst[:, 3, gi:gi + 1], ALU.subtract, ALU.mult),
                     s_scale, CH * l + c + 1)

            for l in range(NLAYER):
                if l == 0:
                    dve.wait_ge(s_w0e, 1)
                    dve.wait_ge(s_feat0, 16)
                    node_products(0)
                    for gi in range(2):
                        for part in range(3):
                            bounds(0, gi, part)
                    for u in range(SS):
                        make_mask(0, 0, u)
                    dve.wait_ge(s_x0, 16)
                    node_products(1)
                    for u in range(SS, V_AT):
                        make_mask(0, 0, u)
                else:
                    dve.wait_ge(s_oe, 4 * blk(l, 0))
                    for part in range(3):
                        bounds(l, 1, part)
                at = stats_at(l, 2)
                step(dv.tensor_tensor(floor[:, 0:2], gst[:, 0, :], gst[:, 2, :], ALU.add), s_startseq, at + 1)
                step(dv.tensor_tensor(floor[:, 2:3], floor[:, 0:1], floor[:, 1:2], ALU.min), s_startseq, at + 2)
                step(dv.tensor_scalar(v8col[:, :], vucol[:, l % 2, 0, :], 1.0 - ALPHA, None, ALU.mult),
                     s_startseq, at + 3)
                step(dv.tensor_scalar(v2col[:, :], vucol[:, l % 2, 0, :], ALPHA, None, ALU.mult),
                     s_startseq, at + 4)
                for u in range(UNITS) if l == 0 else range(GCH * RT, UNITS):
                    if l == 0 and u + V_AT < UNITS:
                        make_mask(0, 0, u + V_AT)
                    if u % RT == 0:
                        scale(l, u // RT)
                    if l == 0:
                        dve.wait_ge(s_mask, u + 1)
                    if l * NB * UNITS + u > 1:
                        dve.wait_ge(s_unit, blk(l, 0) * UNITS + u - 1)
                    unit_min(l, 0, 0, u)
                for part in range(3):
                    head(l, 0, 0, part)
                add_u(l, 0, 0)

                def body(b, par, head_, tail_):
                    for t in range(NT):
                        for u in (UNIT_AT_0 if l == 0 else UNIT_AT).get(t, []) if head_ else []:
                            dve.wait_ge(s_unit, blk(l, b + 1) * UNITS + u - 1)
                        if t == 0:
                            dve.wait_ge(s_ua, blk(l, b) + 1)
                        if t not in ON_ACT[l]:
                            start_scores(l, b, t, par)
                        if tail_:
                            tail_step(l, b - 1, 1 - par, t)
                        if not head_ and l < NLAYER - 1:
                            if t in (T_BOUNDS, T_BOUNDS + 2, T_BOUNDS + 4):
                                if t == T_BOUNDS:
                                    dve.wait_ge(s_oe, 4 * (blk(l, 0) + GB))
                                bounds(l + 1, 0, (t - T_BOUNDS) // 2)
                            for u in EARLY_AT.get(t, []):
                                if u % RT == 0:
                                    scale(l + 1, u // RT)
                                dve.wait_ge(s_unit, blk(l + 1, 0) * UNITS + u - 1)
                                unit_min(l + 1, 0, 0, u)
                        if head_:
                            if l == 0:
                                for u in range(UNITS + 1):
                                    if t == u * T_UNITS // UNITS:
                                        if u > 0:
                                            dve.wait_ge(s_mask, (b + 1) * UNITS + u)
                                        if u < UNITS:
                                            make_mask(b + 1, 1 - par, u)
                                        else:
                                            dv.memset(st[:, 8:9], 0.0)
                                        if u > 0:
                                            unit_min(l, b + 1, 1 - par, u - 1)
                            else:
                                for u in UNIT_AT.get(t, []):
                                    unit_min(l, b + 1, 1 - par, u)
                            if T_HEAD <= t < T_HEAD + 3:
                                head(l, b + 1, 1 - par, t - T_HEAD)
                            if t == T_UA:
                                add_u(l, b + 1, 1 - par)

                blocks(dve, body)
                for t in range(NT):
                    tail_step(l, NB - 1, 1, t)


_INS = ["x", "adj", "L0_gnn_entity_embs", "L0_gnn_W", "L0_gnn_a", "L1_gnn_W", "L1_gnn_lin_w", "L1_gnn_lin_b",
        "L1_gnn_attn", "L1_gnn_mlp_w", "L1_gnn_mlp_b"]


def kernel(**inputs):
    import numpy as _np
    import concourse.bacc as _bacc
    from concourse import mybir as _mybir
    from concourse.bass_utils import run_bass_kernel_spmd as _run

    nc = _bacc.Bacc("TRN2", target_bir_lowering=False, num_devices=1)
    arrays, args = {}, []
    for name in _INS:
        a = _np.ascontiguousarray(inputs[name])
        arrays[f"in_{name}_dram"] = a
        args.append(nc.dram_tensor(f"in_{name}_dram", a.shape, _mybir.dt.from_np(a.dtype), kind="ExternalInput").ap())
    args.append(nc.dram_tensor("out_0_dram", (N, C), F32, kind="ExternalOutput").ap())
    build(nc, *args)
    r = _run(nc, [arrays], core_ids=[0])
    return r.results[0]["out_0_dram"]
```
